# Optimizing a Trainium2 kernel written in Bass

```python
import numpy as np
import jax
import jax.numpy as jnp

def _softmax(x, axis=-1):
    return jax.nn.softmax(x, axis=axis)

def _gelu(x):
    return jax.nn.gelu(x, approximate=True)

def _silu(x):
    return jax.nn.silu(x)

def _sigmoid(x):
    return jax.nn.sigmoid(x)

def _layernorm(x, axis=-1, eps=1e-05):
    m = jnp.mean(x, axis=axis, keepdims=True)
    v = jnp.var(x, axis=axis, keepdims=True)
    return (x - m) / jnp.sqrt(v + eps)

def _scatter_add(tgt, idx, src, axis=0):
    return tgt.at[idx].add(src)

def _segment_sum(src, seg, n):
    return jax.ops.segment_sum(src, seg, n)
kernel_name = 'mk_seq_preln_d1_jaxref_r4_123956'

def setup_inputs(seed: int=0):
    np.random.seed(seed)
    _w = jnp.asarray

    def _L0_attn_setup():
        import jax, jax.numpy as jnp
        import numpy as np
        B, S, D, H = (4, 1024, 256, 16)
        DH = D // H
        key = jax.random.key(seed)
        ks = jax.random.split(key, 6)
        std = 0.02
        return {'hidden_states': jax.random.normal(ks[0], (B, S, D), jnp.float32), 'Wq': jax.random.normal(ks[1], (D, D), jnp.float32) * std, 'bq': jnp.zeros((D,), jnp.float32), 'Wqa': jax.random.normal(ks[2], (D, H), jnp.float32) * std, 'bqa': jnp.zeros((H,), jnp.float32), 'Wk': jax.random.normal(ks[3], (D, D), jnp.float32) * std, 'bk': jnp.zeros((D,), jnp.float32), 'Wka': jax.random.normal(ks[4], (D, H), jnp.float32) * std, 'bka': jnp.zeros((H,), jnp.float32), 'Wt': jax.random.normal(ks[5], (D, D), jnp.float32) * std, 'bt': jnp.zeros((D,), jnp.float32)}
    _L0_attn_in = _L0_attn_setup()

    def _L0_ffn_setup():
        import jax, jax.numpy as jnp
        import numpy as np
        D, H, O, E, TOPK = (256, 1024, 256, 8, 2)
        B, S = (4, 256)
        key = jax.random.key(seed)
        ks = jax.random.split(key, 12)
        std = 0.02
        return {'hidden_states': jax.random.normal(ks[0], (B, S, D), dtype=jnp.float32), 'norm_weight': jnp.ones((D,), dtype=jnp.float32), 'router_w': jax.random.normal(ks[1], (E, D), dtype=jnp.float32) * std, 'sw1': jax.random.normal(ks[2], (D, H), dtype=jnp.float32) * (1.0 / np.sqrt(D)), 'sb1': jnp.zeros((H,), dtype=jnp.float32), 'sw2': jax.random.normal(ks[3], (H, O), dtype=jnp.float32) * (1.0 / np.sqrt(H)), 'sb2': jnp.zeros((O,), dtype=jnp.float32), 'ew1': jax.random.normal(ks[4], (E, D, H), dtype=jnp.float32) * (1.0 / np.sqrt(D)), 'eb1': jnp.zeros((E, H), dtype=jnp.float32), 'ew2': jax.random.normal(ks[5], (E, H, O), dtype=jnp.float32) * (1.0 / np.sqrt(H)), 'eb2': jnp.zeros((E, O), dtype=jnp.float32)}
    _L0_ffn_in = _L0_ffn_setup()
    _d = {'L0_attn_hidden_states': _L0_attn_in['hidden_states'], 'L0_attn_Wq': _L0_attn_in['Wq'], 'L0_attn_bq': _L0_attn_in['bq'], 'L0_attn_Wqa': _L0_attn_in['Wqa'], 'L0_attn_bqa': _L0_attn_in['bqa'], 'L0_attn_Wk': _L0_attn_in['Wk'], 'L0_attn_bk': _L0_attn_in['bk'], 'L0_attn_Wka': _L0_attn_in['Wka'], 'L0_attn_bka': _L0_attn_in['bka'], 'L0_attn_Wt': _L0_attn_in['Wt'], 'L0_attn_bt': _L0_attn_in['bt'], 'L0_ffn_norm_weight': _L0_ffn_in['norm_weight'], 'L0_ffn_router_w': _L0_ffn_in['router_w'], 'L0_ffn_sw1': _L0_ffn_in['sw1'], 'L0_ffn_sb1': _L0_ffn_in['sb1'], 'L0_ffn_sw2': _L0_ffn_in['sw2'], 'L0_ffn_sb2': _L0_ffn_in['sb2'], 'L0_ffn_ew1': _L0_ffn_in['ew1'], 'L0_ffn_eb1': _L0_ffn_in['eb1'], 'L0_ffn_ew2': _L0_ffn_in['ew2'], 'L0_ffn_eb2': _L0_ffn_in['eb2']}
    _x0 = _d['L0_attn_hidden_states']
    _d['L0_attn_hidden_states'] = jax.random.normal(jax.random.fold_in(jax.random.key(seed), 1), (2, 2048, 256), dtype=_x0.dtype)
    del _x0
    return _d

def reference(L0_attn_hidden_states, L0_attn_Wq, L0_attn_bq, L0_attn_Wqa, L0_attn_bqa, L0_attn_Wk, L0_attn_bk, L0_attn_Wka, L0_attn_bka, L0_attn_Wt, L0_attn_bt, L0_ffn_norm_weight, L0_ffn_router_w, L0_ffn_sw1, L0_ffn_sb1, L0_ffn_sw2, L0_ffn_sb2, L0_ffn_ew1, L0_ffn_eb1, L0_ffn_ew2, L0_ffn_eb2):

    def _L0_attn_ref(hidden_states, Wq, bq, Wqa, bqa, Wk, bk, Wka, bka, Wt, bt):
        import jax, jax.numpy as jnp
        import numpy as np
        B, S, D, H = (4, 1024, 256, 16)
        DH = D // H
        b, s, dm = hidden_states.shape
        h = bqa.shape[0]
        dh = dm // h
        scale = 1.0 / np.sqrt(dh)
        mixed_q = hidden_states @ Wq + bq
        mixed_k = hidden_states @ Wk + bk
        q_score = (mixed_q @ Wqa + bqa) * scale
        q_w = jax.nn.softmax(q_score, axis=1)
        pooled_q = jnp.einsum('bsh,bshd->bhd', q_w, mixed_q.reshape(b, s, h, dh))
        pooled_q = pooled_q.reshape(b, 1, dm)
        mixed_qk = mixed_k * pooled_q
        k_score = (mixed_qk @ Wka + bka) * scale
        k_w = jax.nn.softmax(k_score, axis=1)
        pooled_k = jnp.einsum('bsh,bshd->bhd', k_w, mixed_qk.reshape(b, s, h, dh))
        wv = pooled_k[:, None, :, :] * mixed_q.reshape(b, s, h, dh)
        wv = wv.reshape(b, s, dm)
        return wv @ Wt + bt + mixed_q

    def _L0_ffn_ref(hidden_states, norm_weight, router_w, sw1, sb1, sw2, sb2, ew1, eb1, ew2, eb2):
        import jax, jax.numpy as jnp
        import numpy as np
        D, H, O, E, TOPK = (256, 1024, 256, 8, 2)
        B, S = (4, 256)
        b, s, d = hidden_states.shape
        var = jnp.mean(jnp.square(hidden_states), axis=-1, keepdims=True)
        normed = hidden_states * jax.lax.rsqrt(var + 1e-08) * norm_weight
        shared = jnp.maximum(normed @ sw1 + sb1, 0.0) @ sw2 + sb2
        flat = normed.reshape(-1, d)
        T = flat.shape[0]
        probs = jax.nn.sigmoid(flat @ router_w.T)
        scores, idx = jax.lax.top_k(probs, TOPK)
        w = scores / (jnp.sum(scores, axis=-1, keepdims=True) + 1e-06)
        comb = jnp.zeros((T, E), dtype=flat.dtype)
        comb = comb.at[jnp.arange(T)[:, None], idx].add(w)
        h = jnp.maximum(jnp.einsum('td,edh->teh', flat, ew1) + eb1[None, :, :], 0.0)
        eo = jnp.einsum('teh,eho->teo', h, ew2) + eb2[None, :, :]
        routed = jnp.einsum('teo,te->to', eo, comb)
        return shared + routed.reshape(b, s, -1)
    x = L0_attn_hidden_states
    x = x + _L0_attn_ref(_layernorm(x, axis=-1), L0_attn_Wq, L0_attn_bq, L0_attn_Wqa, L0_attn_bqa, L0_attn_Wk, L0_attn_bk, L0_attn_Wka, L0_attn_bka, L0_attn_Wt, L0_attn_bt)
    x = x + _L0_ffn_ref(_layernorm(x, axis=-1), L0_ffn_norm_weight, L0_ffn_router_w, L0_ffn_sw1, L0_ffn_sb1, L0_ffn_sw2, L0_ffn_sb2, L0_ffn_ew1, L0_ffn_eb1, L0_ffn_ew2, L0_ffn_eb2)
    return x

_drawn_inputs = setup_inputs


def setup_inputs(seed=0):
    import zlib

    import numpy as np

    out = dict(_drawn_inputs(seed))
    spreads = {'L0_attn_bq': (0.0, 0.1),
     'L0_attn_bqa': (0.0, 2.0),
     'L0_attn_bk': (0.0, 0.624),
     'L0_attn_bka': (0.0, 2.0),
     'L0_attn_bt': (0.0, 0.1),
     'L0_ffn_norm_weight': (1.0, 0.2),
     'L0_ffn_sb1': (0.0, 0.1),
     'L0_ffn_sb2': (0.0, 0.1),
     'L0_ffn_eb1': (0.0, 0.1),
     'L0_ffn_eb2': (0.0, 0.1)}
    factors = {'L0_attn_Wqa': 47.661, 'L0_attn_Wk': 25.165, 'L0_attn_Wka': 33.281, 'L0_attn_Wt': 5.296}
    for name, (base, spread) in spreads.items():
        noise = np.random.default_rng([zlib.crc32(name.encode()), seed]).standard_normal(out[name].shape)
        drawn = base * np.exp(spread * noise) if base else spread * noise
        out[name] = jnp.asarray(drawn.astype(out[name].dtype))
    for name, factor in factors.items():
        out[name] = (out[name] * factor).astype(out[name].dtype)
    return out
```

```python
from contextlib import ExitStack

import numpy as np

import concourse.bass as bass
from concourse import mybir

ALU = mybir.AluOpType
ACT = mybir.ActivationFunctionType
F32 = mybir.dt.float32
I32 = mybir.dt.int32
U32 = mybir.dt.uint32
X = mybir.AxisListType.X

P = 128
D, KD = 256, 2
H, MH = 1024, 8
E = 8
NH = 16
B, S = 2, 2048
T = B * S
NT = T // P
CH = 8
NC = NT // CH
BLK = 256
NB = (2 * T - E) // BLK + E
NBP = NB + 1
SH = S // BLK
W2 = KD * H
WROW = 2 * W2
EPS_LN, EPS_RMS, EPS_W = 1e-5, 1e-8, 1e-6
SCALE = float(D // NH) ** -0.5
MAXT = S * B // BLK

C_ID, C_TRI, C_ONE = 0, P, 2 * P
C_EYE = 3 * P
C_HM = C_EYE + KD * D
C_IOTA = C_HM + KD * NH
C_SCAN = C_IOTA + NT * E
C_THR = C_SCAN + E * NT
C_BLK = C_THR + E * MAXT
C_HALF = C_BLK + NBP * E
C_ALL = C_HALF + NT
A_WQ, A_WK, A_WT = 0, KD * D, 2 * KD * D
A_WQT, A_WKT = 3 * KD * D, 4 * KD * D
A_WQA = 5 * KD * D
A_WKA = A_WQA + KD * 32
A_BQ = A_WKA + KD * 32
A_BK = A_BQ + KD
A_NW = A_BK + KD
A_RW = A_NW + KD
A_BQA = A_RW + KD * 32
A_BKA = A_BQA + 1
A_ALL = A_BKA + 1


def build(nc, x, consts, attn, bt, wpack, b1pack, b2pack, out):
    with ExitStack() as ctx:
        def sb(name, shape, dt=F32):
            return ctx.enter_context(nc.sbuf_tensor(name, shape, dt))

        def ps(name, shape):
            return ctx.enter_context(nc.psum_tensor(name, shape, F32))

        def sem(name):
            return ctx.enter_context(nc.semaphore(name))

        xs = nc.dram_tensor("expert_in", [NB * BLK, D], F32).ap()
        ys = nc.dram_tensor("expert_out", [NB * BLK, D], F32).ap()

        x_sb = sb("x_sb", [P, NT, D])
        z_sb = sb("z_sb", [P, NT, D])
        xT = sb("xT", [P, KD, T])
        cst = sb("cst", [P, C_ALL])
        att = sb("att", [P, A_ALL])
        bt_bc = sb("bt_bc", [P, D])
        cbc = sb("cbc", [P, B, D])
        bqrep = sb("bqrep", [P, KD, P])
        stats = sb("stats", [P, NT, 6])
        ssum = sb("ssum", [P, NT])
        sdif = sb("sdif", [P, NT])
        sm2 = sb("sm2", [P, NT])
        mean = sb("mean", [P, NT])
        var = sb("var", [P, NT])
        vare = sb("vare", [P, NT])
        rstd = sb("rstd", [P, NT])
        rr = sb("rr", [P, NT])
        rr2 = sb("rr2", [P, NT])
        rr3 = sb("rr3", [P, NT])
        zscale = sb("zscale", [P, NT])
        aq = sb("aq", [P, KD, 32])
        bk_ = sb("bk_", [P, KD, B * 32])
        gk = sb("gk", [P, KD, B, 32])
        prob = sb("prob", [64, S])
        eT = sb("eT", [P, S // P, B * NH])
        pool_sb = sb("pool_sb", [P, KD, B * NH])
        dtmp = sb("dtmp", [P, KD, B, NH])
        dred = sb("dred", [P, KD, B])
        pq = sb("pq", [P, KD, B])
        pk = sb("pk", [P, KD, B])
        small = sb("small", [64, 8])
        pooled = sb("pooled", [64, D])
        fold = sb("fold", [P, 2, KD, B, D])
        gt, mt = fold[:, 0], fold[:, 1]
        pr = sb("pr", [P, NT, E])
        pr2 = sb("pr2", [P, NT, E])
        ra = sb("ra", [P, NT, E])
        oh1 = sb("oh1", [P, NT, E])
        oh2 = sb("oh2", [P, NT, E])
        oh = sb("oh", [P, NT, E])
        top = sb("top", [P, 8, NT])
        tot = sb("tot", [P, E, NT])
        inc = sb("inc", [P, E, NT])
        posm = sb("posm", [P, E, NT])
        blk = sb("blk", [P, 4, E])
        thr = sb("thr", [P, E, MAXT])
        bcmp = sb("bcmp", [P, NBP, E])
        eidf = sb("eidf", [P, NBP])
        eid = sb("eid", [P, NBP], I32)
        pos = sb("pos", [P, 2, NT], U32)
        w = sb("w", [P, 2, WROW])
        b1 = sb("b1", [P, 2, MH])
        b2 = sb("b2", [P, 2, D])
        xin = sb("xin", [P, 2, 2, D])
        xt = sb("xt", [P, 2, KD, BLK])
        hid = sb("hid", [P, MH, BLK])
        yo = sb("yo", [P, 2, 2, D])
        ring = fold[:].rearrange("p a k b d -> p (a k) b d")

        psT = ps("psT", [P, 2, 512])
        psU = ps("psU", [P, 4, 512])
        psD = ps("psD", [P, 2, 512])

        ident = cst[:, C_ID:C_ID + P]
        tri = cst[:, C_TRI:C_TRI + P]
        ones = cst[:, C_ONE:C_ONE + P]
        iota = cst[:, C_IOTA:C_IOTA + NT * E].rearrange("p (t e) -> p t e", e=E)
        wq = att[:, A_WQ:A_WQ + KD * D].rearrange("p (k n) -> p k n", k=KD)
        wk = att[:, A_WK:A_WK + KD * D].rearrange("p (k n) -> p k n", k=KD)
        wt = att[:, A_WT:A_WT + KD * D].rearrange("p (k n) -> p k n", k=KD)
        wqT = att[:, A_WQT:A_WQT + KD * D].rearrange("p (k n) -> p k n", k=KD)
        wkT = att[:, A_WKT:A_WKT + KD * D].rearrange("p (k n) -> p k n", k=KD)
        wqa = att[:, A_WQA:A_WQA + KD * 32].rearrange("p (k n) -> p k n", k=KD)
        wka = att[:, A_WKA:A_WKA + KD * 32].rearrange("p (k n) -> p k n", k=KD)
        rwT = att[:, A_RW:A_RW + KD * 32].rearrange("p (k n) -> p k n", k=KD)
        hm = cst[:, C_HM:C_HM + KD * NH].rearrange("p (k h) -> p k h", k=KD)
        eye = cst[:, C_EYE:C_EYE + KD * D].rearrange("p (k n) -> p k n", k=KD)
        lgT = w[:, 0, 0:1024].rearrange("p (r n) -> p r n", r=2)

        x_rows = x.rearrange("b (t p) d -> p (b t) d", p=P)
        out_rows = out.rearrange("b (t p) d -> p (b t) d", p=P)
        xs_rows = xs.rearrange("(n p) d -> p n d", p=P)
        ys_rows = ys.rearrange("(n p) d -> p n d", p=P)
        xs_zero = xs.rearrange("(p n) d -> p (n d)", p=P)
        ZW = NB * BLK * D // P

        x_loaded = [sem(f"x_loaded{c}") for c in range(NC)]
        cst_loaded, att_loaded, bt_loaded = sem("cst_loaded"), sem("att_loaded"), sem("bt_loaded")
        w_loaded = [sem("w_loaded0"), sem("w_loaded1")]
        b2_loaded = [sem("b2_loaded0"), sem("b2_loaded1")]
        xin_loaded = [sem("xin_loaded0"), sem("xin_loaded1")]
        y_stored = [sem("y_stored0"), sem("y_stored1")]
        zero_made, zero_filled = sem("zero_made"), sem("zero_filled")
        dve_step, pool_step = sem("dve_step"), sem("pool_step")
        var_ready, rstd_ready = sem("var_ready"), sem("rstd_ready")
        xn_ready, xnT_ps, xnT_ready = sem("xn_ready"), sem("xnT_ps"), sem("xnT_ready")
        fold_ps, fold_sb = sem("fold_ps"), sem("fold_sb")
        score_ps, bias_ready, prob_ready = sem("score_ps"), sem("bias_ready"), sem("prob_ready")
        pooled_div, pooledT_ps = sem("pooled_div"), sem("pooledT_ps")
        rsum_ready, probT_ps, probT_ready = sem("rsum_ready"), sem("probT_ps"), sem("probT_ready")
        pooled_ps, pooled_sb = sem("pooled_ps"), sem("pooled_sb")
        headed_ps, headed_sb = sem("headed_ps"), sem("headed_sb")
        mix_ready, m_ps, m_ready, cbc_ready = sem("mix_ready"), sem("m_ps"), sem("m_ready"), sem("cbc_ready")
        xc_ready, proj_ps, x1_ready = sem("xc_ready"), sem("proj_ps"), sem("x1_ready")
        var2_ready, zscale_ready = sem("var2_ready"), sem("zscale_ready")
        z_ready, zT_ps, zT_ready = sem("z_ready"), sem("zT_ps"), sem("zT_ready")
        logits_sb, lgT_ps = sem("logits_sb"), sem("lgT_ps")
        logits_ps, el_ready, onehot_ready = sem("logits_ps"), sem("el_ready"), sem("onehot_ready")
        rank_ps, routed = sem("rank_ps"), sem("routed")
        scattered = sem("scattered")
        up_ps, hid_ready, down_done, out_done = sem("up_ps"), sem("hid_ready"), sem("down_done"), sem("out_done")
        blkT_ps, blkT_ready = sem("blkT_ps"), sem("blkT_ready")
        bias_added = sem("bias_added")
        gathered = [sem(f"gathered{r}") for r in range(4)]
        combined, out_stored = sem("combined"), sem("out_stored")

        block = ctx.enter_context(nc.Block())

        @block.sync
        def _(sp):
            for c in range(NC):
                sp.dma_start(x_sb[:, c * CH:(c + 1) * CH, :],
                             x_rows[:, c * CH:(c + 1) * CH, :]).then_inc(x_loaded[c], 16)
            sp.dma_start(w[:, 1, :], wpack[E]).then_inc(w_loaded[1], 16)
            sp.dma_start(b1[:, 1, :], b1pack[E]).then_inc(w_loaded[1], 16)
            sp.dma_start(b2[:, 1, :], b2pack[E:E + 1, :].to_broadcast([P, D])).then_inc(b2_loaded[1], 16)
            sp.wait_ge(zero_made, 1)
            flat = hid[:].rearrange("p m n -> p (m n)")
            done = 0
            while done < ZW:
                n = min(MH * BLK, ZW - done)
                sp.dma_start(xs_zero[:, done:done + n], flat[:, 0:n]).then_inc(zero_filled, 16)
                done += n

            def weights(j, s):
                e = sp.value_load(eid[0:1, bass.ds(j, 1)], min_val=0, max_val=E - 1)
                sp.dma_start(w[:, s, :], wpack[bass.ds(e, 1)].rearrange("a p n -> (a p) n")).then_inc(w_loaded[s], 16)
                sp.dma_start(b1[:, s, :], b1pack[bass.ds(e, 1)].rearrange("a p n -> (a p) n")).then_inc(w_loaded[s], 16)
                return e

            def rows(j, s):
                sp.dma_start(xin[:, s, :, :], xs_rows[:, bass.ds(2 * j, 2), :]).then_inc(xin_loaded[s], 16)

            def second_bias(e, s):
                sp.dma_start(b2[:, s, :], b2pack[bass.ds(e, 1), :].to_broadcast([P, D])).then_inc(b2_loaded[s], 16)

            def store(j, s):
                sp.dma_start(ys_rows[:, bass.ds(2 * j, 2), :], yo[:, s, :, :]).then_inc(y_stored[s], 16)

            sp.wait_ge(routed, 1)
            e0 = weights(0, 0)
            second_bias(e0, 0)
            sp.wait_ge(scattered, 16 * 2 * NT)
            rows(0, 0)
            rows(1, 1)
            sp.wait_ge(down_done, SH)
            e1 = weights(1, 1)
            sp.wait_ge(bias_added, SH)
            second_bias(e1, 1)

            def step(j, s):
                sp.wait_ge(down_done, SH - 1 + j)
                rows(j, s)
                e = weights(j, s)
                sp.wait_ge(out_done, SH - 1 + j)
                second_bias(e, s)
                store(j - 2, s)

            with sp.Fori(0, (NB - 3) // 2) as i:
                step(2 * i + 2, 0)
                step(2 * i + 3, 1)
            step(NB - 1, 0)
            sp.wait_ge(down_done, SH + NB - 1)
            sp.dma_start(w[:, 1, :], wpack[E]).then_inc(w_loaded[1], 16)
            sp.dma_start(b1[:, 1, :], b1pack[E]).then_inc(w_loaded[1], 16)
            sp.wait_ge(out_done, SH + NB - 1)
            sp.dma_start(b2[:, 1, :], b2pack[E:E + 1, :].to_broadcast([P, D])).then_inc(b2_loaded[1], 16)
            store(NB - 2, 1)
            sp.wait_ge(out_done, SH + NB)
            store(NB - 1, 0)
            with sp.Fori(0, SH) as i:
                for b in range(B):
                    sp.wait_ge(combined, 4 * i + 2 * b + 2)
                    sp.dma_start(out_rows[:, bass.ds(2 * i + b * (NT // B), 2), :],
                                 x_sb[:, bass.ds(2 * i + b * (NT // B), 2), :]).then_inc(out_stored, 16)
            sp.wait_ge(out_stored, 16 * 2 * SH)

        @block.gpsimd
        def _(pool):
            nc.gpsimd.memset(hid[:], 0.0).then_inc(zero_made, 1)
            count = [0]

            def link(ins):
                count[0] += 1
                ins.then_inc(pool_step, 1)
                pool.wait_ge(pool_step, count[0])

            half = cst[:, C_HALF:C_HALF + CH]
            pool.wait_ge(cst_loaded, 16)
            for c in range(NC):
                a, z = c * CH, (c + 1) * CH
                pool.wait_ge(var_ready, c + 1)
                nc.gpsimd.tensor_tensor(rstd[:, a:z], vare[:, a:z], half, ALU.pow).then_inc(rstd_ready, 1)
            pool.wait_ge(cbc_ready, 1)
            pool.wait_ge(xn_ready, NT)
            for c in range(NC + 1):
                if c < NC:
                    for t in range(c * CH, (c + 1) * CH):
                        nc.gpsimd.tensor_tensor(x_sb[:, t, :], x_sb[:, t, :], cbc[:, t // (NT // B), :],
                                                ALU.add).then_inc(xc_ready, 1)
                if c >= 1:
                    a, z = (c - 1) * CH, c * CH
                    pool.wait_ge(var2_ready, c)
                    link(nc.gpsimd.tensor_tensor(rr[:, a:z], vare[:, a:z], half, ALU.pow))
                    link(nc.gpsimd.tensor_tensor(rr2[:, a:z], rr[:, a:z], rr[:, a:z], ALU.mult))
                    link(nc.gpsimd.tensor_tensor(rr2[:, a:z], rr2[:, a:z], var[:, a:z], ALU.mult))
                    link(nc.gpsimd.tensor_scalar(rr2[:, a:z], rr2[:, a:z], EPS_RMS, None, ALU.add))
                    link(nc.gpsimd.tensor_tensor(rr3[:, a:z], rr2[:, a:z], half, ALU.pow))
                    nc.gpsimd.tensor_tensor(zscale[:, a:z], rr3[:, a:z], rr[:, a:z],
                                            ALU.mult).then_inc(zscale_ready, 1)
            pool.wait_ge(zero_filled, 16 * (-(-ZW // (MH * BLK))))
            pool.wait_ge(routed, 1)
            for t in range(NT):
                for k in range(2):
                    nc.gpsimd.indirect_dma_start(
                        xs, bass.IndirectOffsetOnAxis(pos[:, k, t:t + 1], 0), z_sb[:, t, :], None
                    ).then_inc(scattered, 16)
            pool.wait_ge(y_stored[0], 16 * ((NB + 1) // 2))
            pool.wait_ge(y_stored[1], 16 * (NB // 2))
            for n in range(NT):
                i, q = divmod(n, 4)
                t = 2 * i + q % 2 + (q // 2) * (NT // B)
                if n >= 4:
                    pool.wait_ge(combined, n - 3)
                for k in range(2):
                    nc.gpsimd.indirect_dma_start(
                        ring[:, q, k, :], None, ys, bass.IndirectOffsetOnAxis(pos[:, k, t:t + 1], 0)
                    ).then_inc(gathered[q], 16)

        @block.tensor
        def _(pe):
            mm = nc.tensor.matmul

            pe.wait_ge(att_loaded, 16)
            pe.wait_ge(cst_loaded, 16)
            for k in range(KD):
                for n in range(KD):
                    mm(psD[:, 1, 32 * k:32 * k + 32], wqT[:, n, k * P:(k + 1) * P], wqa[:, n, :],
                       start=(n == 0), stop=(n == KD - 1))
            for b in range(B):
                for n in range(KD):
                    last = mm(psD[32 * b:32 * b + 32, 1, 64:65], wqa[:, n, :], att[:, A_BQ + n:A_BQ + n + 1],
                              start=(n == 0), stop=(n == KD - 1))
            last.then_inc(fold_ps, 1)

            for q in range(NT // 2):
                pe.wait_ge(xn_ready, 2 * q + 2)
                if q >= 2:
                    pe.wait_ge(xnT_ready, q - 1)
                for tt in range(2):
                    for k in range(KD):
                        last = nc.tensor.transpose(psT[:, q % 2, k * 256 + tt * P:k * 256 + (tt + 1) * P],
                                                   z_sb[:, 2 * q + tt, k * P:(k + 1) * P], ident)
                last.then_inc(xnT_ps, 1)

            def scores(lhs):
                for g in range(4):
                    for b in range(B):
                        for k in range(KD):
                            last = mm(psU[32 * b:32 * b + 32, g, :], lhs(k, b),
                                      xT[:, k, b * S + g * 512:b * S + (g + 1) * 512],
                                      start=(k == 0), stop=(k == KD - 1))
                last.then_inc(score_ps, 1)

            def pool_tokens(r):
                pe.wait_ge(prob_ready, r + 1)
                for i in range(S // P):
                    last = nc.tensor.transpose(psT[:, i // 8, (i % 8) * 64:(i % 8 + 1) * 64],
                                               prob[:, i * P:(i + 1) * P], ident[0:64, 0:64])
                last.then_inc(probT_ps, 1)
                pe.wait_ge(probT_ready, r + 1)
                for b in range(B):
                    for i in range(S // P):
                        last = mm(psD[32 * b:32 * b + NH, 1, 128:128 + D], eT[:, i, b * NH:(b + 1) * NH],
                                  z_sb[:, b * (S // P) + i, :], start=(i == 0), stop=(i == S // P - 1))
                last.then_inc(pooled_ps, 1)
                pe.wait_ge(pooled_div, r + 1)
                for k in range(KD):
                    for b in range(B):
                        last = nc.tensor.transpose(psT[:, b, k * NH:(k + 1) * NH],
                                                   pooled[32 * b:32 * b + NH, k * P:(k + 1) * P],
                                                   ident[32 * b:32 * b + NH, 32 * b:32 * b + NH])
                last.then_inc(pooledT_ps, 1)
                pe.wait_ge(pooled_sb, r + 1)
                wmat = (wq, wk)[r]
                for n in range(KD):
                    for k in range(KD):
                        last = mm(psD[:, 1, 384 + 32 * n:416 + 32 * n], wmat[:, k, n * P:(n + 1) * P],
                                  pool_sb[:, k, :], start=(k == 0), stop=(k == KD - 1))
                last.then_inc(headed_ps, 1)

            pe.wait_ge(fold_sb, 1)
            pe.wait_ge(xnT_ready, NT // 2)
            scores(lambda k, b: aq[:, k, :])
            pool_tokens(0)

            pe.wait_ge(headed_sb, 1)
            for k in range(KD):
                for n in range(KD):
                    mm(psD[:, 1, 64 * k:64 * k + 64], wkT[:, n, k * P:(k + 1) * P],
                       gk[:, n, :, :].rearrange("p b h -> p (b h)"), start=(n == 0), stop=(n == KD - 1))
            for b in range(B):
                for n in range(KD):
                    last = mm(psD[32 * b:32 * b + 32, 1, 448:449], gk[:, n, b, :], att[:, A_BK + n:A_BK + n + 1],
                              start=(n == 0), stop=(n == KD - 1))
            last.then_inc(fold_ps, 1)
            pe.wait_ge(fold_sb, 2)
            scores(lambda k, b: bk_[:, k, 32 * b:32 * b + 32])
            pool_tokens(1)

            pe.wait_ge(mix_ready, 1)
            for b in range(B):
                for k in range(KD):
                    for n in range(KD):
                        mm(psT[:, b, k * D:(k + 1) * D], wqT[:, n, k * P:(k + 1) * P], gt[:, n, b, :],
                           start=(n == 0), stop=(n == KD - 1))
                for n in range(KD):
                    last = mm(psD[:, 1, b * D:(b + 1) * D], bqrep[:, n, :], gt[:, n, b, :],
                              start=(n == 0), stop=(n == KD - 1))
            last.then_inc(m_ps, 1)
            pe.wait_ge(m_ready, 1)

            def project(q):
                if q >= 4:
                    pe.wait_ge(x1_ready, q - 3)
                for tt in range(2):
                    t = 2 * q + tt
                    for k in range(KD):
                        last = mm(psU[:, q % 4, tt * D:(tt + 1) * D], xT[:, k, t * P:(t + 1) * P],
                                  mt[:, k, t // (NT // B), :], start=(k == 0), stop=(k == KD - 1))
                last.then_inc(proj_ps, 1)

            def turn_z(q):
                pe.wait_ge(z_ready, 2 * q + 2)
                if q >= 2:
                    pe.wait_ge(zT_ready, q - 1)
                for tt in range(2):
                    for k in range(KD):
                        last = nc.tensor.transpose(psT[:, q % 2, k * 256 + tt * P:k * 256 + (tt + 1) * P],
                                                   z_sb[:, 2 * q + tt, k * P:(k + 1) * P], ident)
                last.then_inc(zT_ps, 1)

            def router(g):
                pe.wait_ge(zT_ready, 2 * g + 2)
                o = 32 * (g % 4)
                for k in range(KD):
                    last = mm(psD[o:o + 32, g // 4, :], rwT[:, k, :], xT[:, k, g * 512:(g + 1) * 512],
                              start=(k == 0), stop=(k == KD - 1))
                if g % 4 == 3:
                    last.then_inc(logits_ps, 1)

            QC = CH // 2
            for c in range(NC + 1):
                if c < NC:
                    for q in range(c * QC, (c + 1) * QC):
                        project(q)
                if c >= 1:
                    for q in range((c - 1) * QC, c * QC):
                        turn_z(q)
                    if c == 1:
                        pe.wait_ge(cbc_ready, 1)
                    router(2 * c - 2)
                    router(2 * c - 1)
            for r in range(2):
                pe.wait_ge(logits_sb, r + 1)
                for i in range(4):
                    last = nc.tensor.transpose(psT[:, r, i * P:(i + 1) * P], lgT[:, r, i * P:(i + 1) * P], ident)
                last.then_inc(lgT_ps, 1)

            pe.wait_ge(onehot_ready, 1)
            ohf = oh[:].rearrange("p t e -> p (t e)")
            mm(psT[:, 0, 0:NT * E], tri, ohf, start=True, stop=True)
            mm(psT[:, 0, NT * E:2 * NT * E], ones, ohf, start=True, stop=True).then_inc(rank_ps, 1)

            def up(s, moving):
                for m in range(MH):
                    for k in range(KD):
                        last = mm(psU[:, m // 2, (m % 2) * BLK:(m % 2 + 1) * BLK],
                                  w[:, s, k * H + m * P:k * H + (m + 1) * P], moving(k),
                                  start=(k == 0), stop=(k == KD - 1))
                    if m % 2:
                        last.then_inc(up_ps, 1)

            def down(g, s, bank, first=False):
                if not first:
                    pe.wait_ge(out_done, g - 1)
                for half in range(2):
                    for c in range(MH):
                        if half == 0:
                            pe.wait_ge(hid_ready, g * MH + c + 1)
                        last = mm(psD[:, bank, half * D:(half + 1) * D],
                                  hid[:, c, half * P:(half + 1) * P],
                                  w[:, s, W2 + c * D:W2 + (c + 1) * D], start=(c == 0), stop=(c == MH - 1))
                last.then_inc(down_done, 1)

            def shared(i, g, bank, first=False):
                up(1, lambda k: xT[:, k, bass.ds(i * BLK, BLK)])
                down(g, 1, bank, first)

            pe.wait_ge(w_loaded[1], 32)
            shared(0, 0, 0, True)
            shared(1, 1, 1, True)
            with pe.Fori(1, SH // 2) as i:
                shared(2 * i, 2 * i, 0)
                shared(2 * i + 1, 2 * i + 1, 1)

            def turn_block(j, s, uses):
                pe.wait_ge(xin_loaded[s], 16 * uses)
                for half in range(2):
                    for k in range(KD):
                        last = nc.tensor.transpose(psT[:, s, k * BLK + half * P:k * BLK + (half + 1) * P],
                                                   xin[:, s, half, k * P:(k + 1) * P], ident)
                last.then_inc(blkT_ps, 1)

            def expert(j, s, uses, next_uses):
                pe.wait_ge(blkT_ready, j + 1)
                pe.wait_ge(w_loaded[s], 32 * uses)
                up(s, lambda k: xt[:, s, k, :])
                if next_uses is not None:
                    turn_block(j + 1, 1 - s, next_uses)
                down(SH + j, s, s)

            turn_block(0, 0, 1)
            with pe.Fori(0, NB // 2) as i:
                expert(2 * i, 0, i + 1, i + 1)
                expert(2 * i + 1, 1, i + 2, i + 2)
            expert(NB - 1, 0, NB // 2 + 1, None)

            pe.wait_ge(w_loaded[1], 32 * (NB // 2 + 2))
            with pe.Fori(0, SH // 2) as i:
                shared(2 * i + SH, 2 * i + SH + NB, 1)
                shared(2 * i + SH + 1, 2 * i + SH + NB + 1, 0)

        @block.scalar
        def _(act):
            act.dma_start(att[:, :], attn).then_inc(att_loaded, 16)
            act.dma_start(cst[:, :], consts).then_inc(cst_loaded, 16)
            act.dma_start(bt_bc[:, :], bt.to_broadcast([P, D])).then_inc(bt_loaded, 16)
            copy = ACT.Copy
            for q in range(NT // 2):
                act.wait_ge(xnT_ps, q + 1)
                nc.scalar.activation(xT[:, :, q * 256:(q + 1) * 256],
                                     psT[:, q % 2, :].rearrange("p (k n) -> p k n", k=KD), copy).then_inc(xnT_ready, 1)
            for r in range(2):
                act.wait_ge(bias_ready, r + 1)
                nc.scalar.activation(prob[:, :], psU[0:64, :, :].rearrange("p g n -> p (g n)"), ACT.Exp,
                                     bias=small[:, 4:5], scale=SCALE,
                                     accum_out=small[:, 5:6]).then_inc(prob_ready, 1)
                act.wait_ge(probT_ps, r + 1)
                nc.scalar.activation(
                    eT[:].rearrange("p i (b h) -> p i b h", b=B),
                    psT[:].rearrange("p a (i b h) -> p (a i) b h", b=B, h=32)[:, :, :, 0:NH], copy).then_inc(probT_ready, 1)
                act.wait_ge(pooled_ps, r + 1)
                act.wait_ge(rsum_ready, r + 1)
                for b in range(B):
                    own = slice(32 * b, 32 * b + NH)
                    last = nc.scalar.activation(pooled[own, :], psD[own, 1, 128:128 + D], copy, scale=small[own, 6:7])
                last.then_inc(pooled_div, 1)
                act.wait_ge(pooledT_ps, r + 1)
                nc.scalar.activation(pool_sb[:].rearrange("p k (b h) -> p k b h", b=B),
                                     psT[:, :, 0:KD * NH].rearrange("p b (k h) -> p k b h", k=KD), copy).then_inc(pooled_sb, 1)
            act.wait_ge(m_ps, 1)
            for b in range(B):
                last = nc.scalar.activation(mt[:, :, b, :], psT[:, b, :].rearrange("p (k n) -> p k n", k=KD), copy)
            last.then_inc(m_ready, 1)
            for q in range(NT // 2):
                act.wait_ge(zT_ps, q + 1)
                for k in range(KD):
                    last = nc.scalar.activation(xT[:, k, q * 256:(q + 1) * 256], psT[:, q % 2, k * 256:(k + 1) * 256],
                                                copy, scale=att[:, A_NW + k:A_NW + k + 1])
                last.then_inc(zT_ready, 1)
                if q % 8 == 7 and q > 8 or q == 11:
                    r = q // 8 if q % 8 == 7 else 0
                    act.wait_ge(logits_ps, r + 1)
                    nc.scalar.activation(lgT[:, r, :], psD[:, r, :], copy).then_inc(logits_sb, 1)
            for r in range(2):
                act.wait_ge(lgT_ps, r + 1)
                nc.scalar.activation(
                    pr[:, r * 16:(r + 1) * 16, :].rearrange("p (g i) e -> p i g e", g=4),
                    psT[:, r, :].rearrange("p (i g e) -> p i g e", i=4, g=4)[:, :, :, 0:E],
                    ACT.Exp, scale=-1.0).then_inc(el_ready, 1)

            def relus(g, s):
                for m in range(MH):
                    if m % 2 == 0:
                        act.wait_ge(up_ps, g * (MH // 2) + m // 2 + 1)
                    nc.scalar.activation(hid[:, m, :], psU[:, m // 2, (m % 2) * BLK:(m % 2 + 1) * BLK], ACT.Relu,
                                         bias=b1[:, s, m:m + 1]).then_inc(hid_ready, 1)

            def block_rows(j, s):
                act.wait_ge(blkT_ps, j + 1)
                for k in range(KD):
                    last = nc.scalar.activation(xt[:, s, k, :], psT[:, s, k * BLK:(k + 1) * BLK], copy,
                                                scale=att[:, A_NW + k:A_NW + k + 1])
                last.then_inc(blkT_ready, 1)

            act.wait_ge(zero_filled, 16 * (-(-ZW // (MH * BLK))))
            with act.Fori(0, SH) as i:
                relus(i, 1)
            block_rows(0, 0)
            with act.Fori(0, NB // 2) as i:
                relus(2 * i + SH, 0)
                block_rows(2 * i + 1, 1)
                relus(2 * i + SH + 1, 1)
                block_rows(2 * i + 2, 0)
            relus(SH + NB - 1, 0)
            with act.Fori(0, SH) as i:
                relus(i + SH + NB, 1)

        @block.vector
        def _(dve):
            count = [0]

            def link(ins):
                count[0] += 1
                ins.then_inc(dve_step, 1)
                dve.wait_ge(dve_step, count[0])

            V = nc.vector

            def moments(c, eps, ready):
                a, z = c * CH, (c + 1) * CH
                st = stats[:, a:z, :]
                V.tensor_tensor(ssum[:, a:z], st[:, :, 1], st[:, :, 4], ALU.add)
                V.tensor_tensor(sm2[:, a:z], st[:, :, 2], st[:, :, 5], ALU.add)
                link(V.tensor_tensor(sdif[:, a:z], st[:, :, 1], st[:, :, 4], ALU.subtract))
                V.tensor_scalar(mean[:, a:z], ssum[:, a:z], 0.5, None, ALU.mult)
                V.tensor_scalar(sm2[:, a:z], sm2[:, a:z], 1.0 / D, None, ALU.mult)
                link(V.scalar_tensor_tensor(sdif[:, a:z], sdif[:, a:z], 0.25, sdif[:, a:z], ALU.mult, ALU.mult))
                link(V.tensor_tensor(var[:, a:z], sdif[:, a:z], sm2[:, a:z], ALU.add))
                V.tensor_scalar(vare[:, a:z], var[:, a:z], eps, None, ALU.add).then_inc(ready, 1)

            def normalise(c):
                dve.wait_ge(rstd_ready, c + 1)
                for t in range(c * CH, (c + 1) * CH):
                    V.tensor_scalar(z_sb[:, t, :], x_sb[:, t, :], mean[:, t:t + 1], rstd[:, t:t + 1],
                                    ALU.subtract, ALU.mult).then_inc(xn_ready, 1)

            for c in range(NC):
                dve.wait_ge(x_loaded[c], 16)
                for t in range(c * CH, (c + 1) * CH):
                    last = V.bn_stats(stats[:, t, :], x_sb[:, t, :])
                link(last)
                moments(c, EPS_LN, var_ready)
                if c >= 1:
                    normalise(c - 1)
            dve.wait_ge(fold_ps, 1)
            V.tensor_copy(aq[:].rearrange("p k h -> p (k h)"), psD[:, 1, 0:64])
            V.tensor_tensor(small[:, 0:1], psD[0:64, 1, 64:65], att[0:64, A_BQA:A_BQA + 1],
                            ALU.add).then_inc(fold_sb, 1)
            normalise(NC - 1)
            dve.wait_ge(bt_loaded, 16)
            for n in range(KD):
                V.tensor_scalar(bqrep[:, n, :], ones, att[:, A_BQ + n:A_BQ + n + 1], None, ALU.mult)

            def softmax(r):
                dve.wait_ge(score_ps, r + 1)
                link(V.tensor_reduce(small[:, 1:2], psU[0:64, :, :].rearrange("p g n -> p (g n)"), X, ALU.max))
                link(V.tensor_tensor(small[:, 2:3], small[:, 1:2], small[:, 0:1], ALU.add))
                link(V.tensor_tensor(small[:, 3:4], small[:, 0:1], small[:, 2:3], ALU.subtract))
                V.tensor_scalar(small[:, 4:5], small[:, 3:4], SCALE, None, ALU.mult).then_inc(bias_ready, 1)
                dve.wait_ge(prob_ready, r + 1)
                V.reciprocal(small[:, 6:7], small[:, 5:6]).then_inc(rsum_ready, 1)

            def heads(r):
                dve.wait_ge(headed_ps, r + 1)
                for n in range(KD):
                    src = psD[:, 1, 384 + 32 * n:416 + 32 * n].rearrange("p (b h) -> p b h", b=B)
                    last = V.tensor_tensor(dtmp[:, n, :, :], src, hm[:, n:n + 1, :].to_broadcast([P, B, NH]), ALU.mult)
                link(last)
                link(V.tensor_reduce(dred[:], dtmp[:], X, ALU.add))

            softmax(0)
            heads(0)
            for n in range(KD):
                last = V.tensor_scalar(pq[:, n, :], dred[:, n, :], att[:, A_BQ + n:A_BQ + n + 1], None, ALU.add)
            link(last)
            for n in range(KD):
                for b in range(B):
                    last = V.tensor_scalar(gk[:, n, b, :], wka[:, n, :], pq[:, n, b:b + 1], None, ALU.mult)
            last.then_inc(headed_sb, 1)
            dve.wait_ge(fold_ps, 2)
            V.tensor_copy(bk_[:].rearrange("p k h -> p (k h)"), psD[:, 1, 0:128])
            V.tensor_tensor(small[:, 0:1], psD[0:64, 1, 448:449], att[0:64, A_BKA:A_BKA + 1],
                            ALU.add).then_inc(fold_sb, 1)
            dve.wait_ge(fold_sb, 2)
            softmax(1)
            heads(1)
            for n in range(KD):
                last = V.tensor_scalar(dred[:, n, :], dred[:, n, :], att[:, A_BK + n:A_BK + n + 1], None, ALU.add)
            link(last)
            link(V.tensor_tensor(pk[:], dred[:], pq[:], ALU.mult))
            for n in range(KD):
                for b in range(B):
                    last = V.scalar_tensor_tensor(gt[:, n, b, :], wt[:, n, :], pk[:, n, b:b + 1], eye[:, n, :],
                                                  ALU.mult, ALU.add)
            last.then_inc(mix_ready, 1)
            dve.wait_ge(m_ps, 1)
            for b in range(B):
                last = V.tensor_tensor(cbc[:, b, :], psD[:, 1, b * D:(b + 1) * D], bt_bc[:, :], ALU.add)
            last.then_inc(cbc_ready, 1)

            QC = CH // 2
            for c in range(NC + 1):
                if c < NC:
                    for q in range(c * QC, (c + 1) * QC):
                        dve.wait_ge(proj_ps, q + 1)
                        dve.wait_ge(xc_ready, 2 * q + 2)
                        pair = x_sb[:, 2 * q:2 * q + 2, :]
                        V.tensor_tensor(pair, psU[:, q % 4, :].rearrange("p (t n) -> p t n", t=2), pair,
                                        ALU.add).then_inc(x1_ready, 1)
                        dve.wait_ge(x1_ready, q + 1)
                        for t in (2 * q, 2 * q + 1):
                            last = V.bn_stats(stats[:, t, :], x_sb[:, t, :])
                    link(last)
                    moments(c, EPS_LN, var2_ready)
                if c >= 1:
                    dve.wait_ge(zscale_ready, c)
                    for t in range((c - 1) * CH, c * CH):
                        V.tensor_scalar(z_sb[:, t, :], x_sb[:, t, :], mean[:, t:t + 1], zscale[:, t:t + 1],
                                        ALU.subtract, ALU.mult).then_inc(z_ready, 1)

            def over_e(ap):
                return ap.rearrange("p (t o) -> p t o", o=1).to_broadcast([P, NT, E])

            def flat(tensor):
                return tensor[:].rearrange("p t e -> p (t e)")

            dve.wait_ge(el_ready, 2)
            link(V.tensor_scalar(flat(pr), flat(pr), 1.0, None, ALU.add))
            link(V.reciprocal(flat(pr), flat(pr)))

            def best(src, row, onehot):
                link(V.tensor_reduce(top[:, row, :], src[:], X, ALU.max))
                link(V.tensor_tensor(ra[:], src[:], over_e(top[:, row, :]), ALU.is_equal))
                link(V.scalar_tensor_tensor(flat(ra), flat(ra), -float(E), iota.rearrange("p t e -> p (t e)"),
                                            ALU.mult, ALU.add))
                link(V.tensor_reduce(top[:, row + 1, :], ra[:], X, ALU.min))
                link(V.tensor_scalar(top[:, row + 1, :], top[:, row + 1, :], float(E), None, ALU.add))
                link(V.tensor_tensor(onehot[:], iota, over_e(top[:, row + 1, :]), ALU.is_equal))

            best(pr, 0, oh1)
            link(V.scalar_tensor_tensor(flat(pr2), flat(oh1), -2.0, flat(pr), ALU.mult, ALU.add))
            best(pr2, 2, oh2)
            V.tensor_tensor(flat(oh), flat(oh1), flat(oh2), ALU.add).then_inc(onehot_ready, 1)
            link(V.tensor_tensor(top[:, 4, :], top[:, 0, :], top[:, 2, :], ALU.add))
            link(V.tensor_scalar(top[:, 4, :], top[:, 4, :], EPS_W, None, ALU.add))
            link(V.reciprocal(top[:, 5, :], top[:, 4, :]))
            V.tensor_tensor(top[:, 6, :], top[:, 0, :], top[:, 5, :], ALU.mult)
            link(V.tensor_tensor(top[:, 7, :], top[:, 2, :], top[:, 5, :], ALU.mult))
            dve.wait_ge(rank_ps, 1)
            link(V.tensor_copy(tot[:], psT[:, 0, NT * E:2 * NT * E].rearrange("p (t e) -> p e t", e=E)))
            link(V.tensor_tensor_scan(inc[:].rearrange("p e t -> p (e t)"), cst[:, C_SCAN:C_SCAN + E * NT],
                                      tot[:].rearrange("p e t -> p (e t)"), 0.0, ALU.mult, ALU.add))
            link(V.tensor_tensor(thr[:], inc[:, :, NT - 1:NT].to_broadcast([P, E, MAXT]),
                                 cst[:, C_THR:C_THR + E * MAXT].rearrange("p (e m) -> p e m", e=E), ALU.is_gt))
            link(V.tensor_reduce(blk[:, 0, :], thr[:], X, ALU.add))
            link(V.tensor_tensor_scan(blk[:, 1, :], ones[:, 0:E], blk[:, 0, :], 0.0, ALU.mult, ALU.add))
            link(V.tensor_tensor(blk[:, 2, :], blk[:, 1, :], blk[:, 0, :], ALU.subtract))
            link(V.tensor_scalar(blk[:, 3, :], blk[:, 2, :], float(BLK), None, ALU.mult))
            link(V.tensor_tensor(posm[:], inc[:], tot[:], ALU.subtract))
            link(V.tensor_tensor(posm[:], posm[:], psT[:, 0, 0:NT * E].rearrange("p (t e) -> p e t", e=E), ALU.add))
            link(V.tensor_tensor(posm[:], posm[:],
                                 blk[:, 3, :].rearrange("p (e o) -> p e o", o=1).to_broadcast([P, E, NT]), ALU.add))
            for k, (onehot, prod) in enumerate(((oh1, ra), (oh2, pr2))):
                link(V.tensor_tensor(prod[:], onehot[:], posm[:].rearrange("p e t -> p t e"), ALU.mult))
                link(V.tensor_reduce(top[:, 4 + k, :], prod[:], X, ALU.add))
                V.tensor_copy(pos[:, k, :], top[:, 4 + k, :])
            link(V.tensor_tensor(bcmp[:], cst[:, C_BLK:C_BLK + NBP * E].rearrange("p (n e) -> p n e", e=E),
                                 blk[:, 1:2, :].to_broadcast([P, NBP, E]), ALU.is_ge))
            link(V.tensor_reduce(eidf[:], bcmp[:], X, ALU.add))
            link(V.tensor_scalar(eidf[:], eidf[:], float(E - 1), None, ALU.min))
            V.tensor_copy(eid[:], eidf[:]).then_inc(routed, 1)

            def shared_out(i, g, bank, base):
                dve.wait_ge(down_done, g + 1)
                pair = x_sb[:, bass.ds(2 * i + base, 2), :]
                V.tensor_tensor(pair, psD[:, bank, :].rearrange("p (t n) -> p t n", t=2), pair,
                                ALU.add).then_inc(out_done, 1)
                dve.wait_ge(out_done, g + 1)
                return V.tensor_tensor(pair, pair, b2[:, 1:2, :].to_broadcast([P, 2, D]), ALU.add)

            dve.wait_ge(b2_loaded[1], 16)
            with dve.Fori(0, SH // 2) as i:
                shared_out(2 * i, 2 * i, 0, 0).then_inc(bias_added, 1)
                shared_out(2 * i + 1, 2 * i + 1, 1, 0).then_inc(bias_added, 1)

            def expert_out(j, s, stored, loads):
                dve.wait_ge(down_done, SH + j + 1)
                if stored is not None:
                    dve.wait_ge(y_stored[s], 16 * stored)
                dve.wait_ge(b2_loaded[s], 16 * loads)
                V.tensor_tensor(yo[:, s, :, :], psD[:, s, :].rearrange("p (t n) -> p t n", t=2),
                                b2[:, s:s + 1, :].to_broadcast([P, 2, D]), ALU.add).then_inc(out_done, 1)

            expert_out(0, 0, None, 1)
            expert_out(1, 1, None, 2)
            with dve.Fori(1, NB // 2) as i:
                expert_out(2 * i, 0, i, i + 1)
                expert_out(2 * i + 1, 1, i, i + 2)
            expert_out(NB - 1, 0, NB // 2, NB // 2 + 1)

            def combine(t, q, i, n):
                dve.wait_ge(gathered[q], 32 * i + 32)
                row = x_sb[:, bass.ds(t, 1), :].rearrange("p a d -> p (a d)")
                link_c(V.scalar_tensor_tensor(row, ring[:, q, 0, :], top[:, 6, bass.ds(t, 1)], row,
                                              ALU.mult, ALU.add), n)
                V.scalar_tensor_tensor(row, ring[:, q, 1, :], top[:, 7, bass.ds(t, 1)], row,
                                       ALU.mult, ALU.add).then_inc(combined, 1)

            base = count[0]

            def link_c(ins, n):
                ins.then_inc(dve_step, 1)
                dve.wait_ge(dve_step, base + n + 1)

            dve.wait_ge(b2_loaded[1], 16 * (NB // 2 + 2))
            with dve.Fori(0, SH // 2) as ii:
                for h in range(2):
                    i = 2 * ii + h
                    combine(2 * i, 0, i, 5 * i)
                    combine(2 * i + 1, 1, i, 5 * i + 1)
                    link_c(shared_out(i, i + SH + NB, 1 - h, NT // B), 5 * i + 2)
                    combine(2 * i + NT // B, 2, i, 5 * i + 3)
                    combine(2 * i + 1 + NT // B, 3, i, 5 * i + 4)


def constants():
    c = np.zeros((P, C_ALL), np.float32)
    p = np.arange(P)
    c[:, C_ID:C_ID + P] = np.eye(P)
    c[:, C_TRI:C_TRI + P] = p[:, None] < p[None, :]
    c[:, C_ONE:C_ONE + P] = 1
    c[:, C_EYE:C_EYE + KD * D] = np.eye(D).reshape(KD, P, D).transpose(1, 0, 2).reshape(P, KD * D)
    feature = np.arange(KD)[None, :, None] * P + p[:, None, None]
    c[:, C_HM:C_HM + KD * NH] = (feature // (D // NH) == np.arange(NH)).reshape(P, KD * NH)
    c[:, C_IOTA:C_IOTA + NT * E] = np.tile(np.arange(E), NT)
    c[:, C_SCAN:C_SCAN + E * NT] = np.tile(np.arange(NT) > 0, E)
    c[:, C_THR:C_THR + E * MAXT] = np.tile(np.arange(MAXT) * BLK, E)
    c[:, C_BLK:C_BLK + NBP * E] = np.repeat(np.arange(NBP), E)
    c[:, C_HALF:C_HALF + NT] = -0.5
    return c


def rows_first(m):
    return np.ascontiguousarray(m.reshape(KD, P, -1).transpose(1, 0, 2).reshape(P, -1))


def kernel(**inputs):
    import concourse.bacc as bacc
    from concourse.bass_utils import run_bass_kernel_spmd

    a = {k: np.asarray(v) for k, v in inputs.items()}
    A, F = "L0_attn_", "L0_ffn_"
    heads = lambda m: np.concatenate([m, np.zeros((D, 32 - NH), np.float32)], 1)
    head_bias = lambda v: np.concatenate([v, np.zeros(16, np.float32)] * 2 + [np.zeros(64, np.float32)])[:, None]
    attn = np.concatenate([
        rows_first(a[A + "Wq"]), rows_first(a[A + "Wk"]), rows_first(a[A + "Wt"]),
        rows_first(a[A + "Wq"].T), rows_first(a[A + "Wk"].T),
        rows_first(heads(a[A + "Wqa"])), rows_first(heads(a[A + "Wka"])),
        rows_first(a[A + "bq"]), rows_first(a[A + "bk"]), rows_first(a[F + "norm_weight"]),
        rows_first(np.concatenate([a[F + "router_w"].T, np.zeros((D, 32 - E), np.float32)], 1)), head_bias(a[A + "bqa"]), head_bias(a[A + "bka"])], 1)
    w1 = np.concatenate([a[F + "ew1"], a[F + "sw1"][None]])
    w2 = np.concatenate([a[F + "ew2"], a[F + "sw2"][None]])
    w1 = w1.reshape(E + 1, KD, P, H).transpose(0, 2, 1, 3).reshape(E + 1, P, W2)
    w2 = w2.reshape(E + 1, MH, P, D).transpose(0, 2, 1, 3).reshape(E + 1, P, W2)
    arrays = {
        "x": a[A + "hidden_states"],
        "consts": constants(),
        "attn": attn,
        "bt": a[A + "bt"][None],
        "wpack": np.concatenate([w1, w2], 2),
        "b1pack": np.concatenate([a[F + "eb1"], a[F + "sb1"][None]]).reshape(E + 1, MH, P).transpose(0, 2, 1),
        "b2pack": np.concatenate([a[F + "eb2"], a[F + "sb2"][None]]),
    }
    nc = bacc.Bacc("TRN2", target_bir_lowering=False, num_devices=1)
    feeds, args = {}, []
    for name, v in arrays.items():
        v = np.ascontiguousarray(v)
        feeds["in_" + name] = v
        args.append(nc.dram_tensor("in_" + name, v.shape, mybir.dt.from_np(v.dtype), kind="ExternalInput").ap())
    out = nc.dram_tensor("out", (B, S, D), F32, kind="ExternalOutput").ap()
    build(nc, *args, out)
    return run_bass_kernel_spmd(nc, [feeds], core_ids=[0]).results[0]["out"]
```

```python
from contextlib import ExitStack

import numpy as np

import concourse.bass as bass
from concourse import mybir

ALU = mybir.AluOpType
ACT = mybir.ActivationFunctionType
F32 = mybir.dt.float32
F32R = mybir.dt.float32r
I32 = mybir.dt.int32
U32 = mybir.dt.uint32
X = mybir.AxisListType.X

P = 128
D, KD = 256, 2
H, MH = 1024, 8
E = 8
NH = 16
B, S = 2, 2048
T = B * S
NT = T // P
CH = 8
NC = NT // CH
BLK = 256
NB = (2 * T - E) // BLK + E
NBP = NB + 1
SH = S // BLK
W2 = KD * H
WROW = 2 * W2
EPS_LN, EPS_RMS, EPS_W = 1e-5, 1e-8, 1e-6
SCALE = float(D // NH) ** -0.5
MAXT = S * B // BLK

C_ID, C_TRI, C_ONE = 0, P, 2 * P
C_EYE = 3 * P
C_HM = C_EYE + KD * D
C_IOTA = C_HM + KD * NH
C_SCAN = C_IOTA + NT * E
C_THR = C_SCAN + E * NT
C_BLK = C_THR + E * MAXT
C_HALF = C_BLK + NBP * E
C_ALL = C_HALF + NT
A_WQ, A_WK, A_WT = 0, KD * D, 2 * KD * D
A_WQT, A_WKT = 3 * KD * D, 4 * KD * D
A_WQA = 5 * KD * D
A_WKA = A_WQA + KD * 32
A_BQ = A_WKA + KD * 32
A_BK = A_BQ + KD
A_RW = A_BK + KD
A_BQA = A_RW + KD * 32
A_BKA = A_BQA + 1
A_ALL = A_BKA + 1


def build(nc, x, consts, attn, norm, bt, wpack, b1pack, b2pack, out):
    with ExitStack() as ctx:
        def sb(name, shape, dt=F32):
            return ctx.enter_context(nc.sbuf_tensor(name, shape, dt))

        def ps(name, shape):
            return ctx.enter_context(nc.psum_tensor(name, shape, F32))

        def sem(name):
            return ctx.enter_context(nc.semaphore(name))

        xs = nc.dram_tensor("expert_in", [NB * BLK, D], F32).ap()
        ys = nc.dram_tensor("expert_out", [NB * BLK, D], F32).ap()

        x_sb = sb("x_sb", [P, NT, D])
        z_sb = sb("z_sb", [P, NT, D])
        cst = sb("cst", [P, C_ALL])
        nw = sb("nw", [P, KD])
        bt_bc = sb("bt_bc", [P, D])
        cbc = sb("cbc", [P, B, D])
        bqrep = sb("bqrep", [P, KD, P])
        stats = sb("stats", [P, NT, 6])
        ssum = sb("ssum", [P, NT])
        sdif = sb("sdif", [P, NT])
        sm2 = sb("sm2", [P, NT])
        mean = sb("mean", [P, NT])
        var = sb("var", [P, NT])
        vare = sb("vare", [P, NT])
        rstd = sb("rstd", [P, NT])
        rr = sb("rr", [P, NT])
        rr2 = sb("rr2", [P, NT])
        rr3 = sb("rr3", [P, NT])
        zscale = sb("zscale", [P, NT])
        aq = sb("aq", [P, KD, 32])
        bk_ = sb("bk_", [P, KD, B * 32])
        gk = sb("gk", [P, KD, B, 32])
        pool_sb = sb("pool_sb", [P, KD, B * NH])
        dtmp = sb("dtmp", [P, KD, B, NH])
        dred = sb("dred", [P, KD, B])
        pq = sb("pq", [P, KD, B])
        pk = sb("pk", [P, KD, B])
        small = sb("small", [64, 8])
        pooled = sb("pooled", [64, D])
        top = sb("top", [P, 8, NT])
        posm = sb("posm", [P, E, NT])
        blk = sb("blk", [P, 4, E])
        thr = sb("thr", [P, E, MAXT])
        bcmp = sb("bcmp", [P, NBP, E])
        eidf = sb("eidf", [P, NBP])
        eid = sb("eid", [P, NBP], I32)
        pos = sb("pos", [P, 2, NT], U32)
        raw = sb("raw", [P, 2, W2])
        whi = sb("whi", [P, 3, W2], F32R)
        wlo = sb("wlo", [P, 3, W2], F32R)
        b1 = sb("b1", [P, 2, MH])
        b2 = sb("b2", [P, 2, D])
        xin = sb("xin", [P, 2, 2, D])
        fold = sb("fold", [P, 2, KD, B, D])
        gt, mt = fold[:, 0], fold[:, 1]
        flat = fold[:].rearrange("p a k b d -> p (a k b d)")
        prob = flat[0:64, :]
        route = flat.rearrange("p (r n) -> p r n", r=8)
        pr, pr2, ra, oh1, oh2, oh = (route[:, i, :].rearrange("p (t e) -> p t e", e=E) for i in range(6))
        tot, inc = (route[:, i, :].rearrange("p (e t) -> p e t", e=E) for i in (6, 7))
        with ExitStack() as early:
            xT = early.enter_context(nc.sbuf_tensor("xT", [P, KD, T], F32))
            att = early.enter_context(nc.sbuf_tensor("att", [P, A_ALL], F32))
        xhi = sb("xhi", [P, 2, KD, BLK], F32R)
        xlo = sb("xlo", [P, 2, KD, BLK], F32R)
        hid = sb("hid", [P, MH, BLK])
        hhi = sb("hhi", [P, MH, BLK], F32R)
        hlo = sb("hlo", [P, MH, BLK], F32R)
        yo = sb("yo", [P, 2, 2, D])
        ring = fold[:].rearrange("p a k b d -> p (a k) b d")

        psT = ps("psT", [P, 2, 512])
        psU = ps("psU", [P, 4, 512])
        psD = ps("psD", [P, 2, 512])

        ident = cst[:, C_ID:C_ID + P]
        tri = cst[:, C_TRI:C_TRI + P]
        ones = cst[:, C_ONE:C_ONE + P]
        iota = cst[:, C_IOTA:C_IOTA + NT * E].rearrange("p (t e) -> p t e", e=E)
        wq = att[:, A_WQ:A_WQ + KD * D].rearrange("p (k n) -> p k n", k=KD)
        wk = att[:, A_WK:A_WK + KD * D].rearrange("p (k n) -> p k n", k=KD)
        wt = att[:, A_WT:A_WT + KD * D].rearrange("p (k n) -> p k n", k=KD)
        wqT = att[:, A_WQT:A_WQT + KD * D].rearrange("p (k n) -> p k n", k=KD)
        wkT = att[:, A_WKT:A_WKT + KD * D].rearrange("p (k n) -> p k n", k=KD)
        wqa = att[:, A_WQA:A_WQA + KD * 32].rearrange("p (k n) -> p k n", k=KD)
        wka = att[:, A_WKA:A_WKA + KD * 32].rearrange("p (k n) -> p k n", k=KD)
        rwT = att[:, A_RW:A_RW + KD * 32].rearrange("p (k n) -> p k n", k=KD)
        hm = cst[:, C_HM:C_HM + KD * NH].rearrange("p (k h) -> p k h", k=KD)
        eye = cst[:, C_EYE:C_EYE + KD * D].rearrange("p (k n) -> p k n", k=KD)
        eT = xin[:, 0, :, :].rearrange("p b n -> p (b n)").rearrange("p (i h) -> p i h", i=S // P)
        lgT = xin[:].rearrange("p a b n -> p (a b n)").rearrange("p (r n) -> p r n", r=2)

        x_rows = x.rearrange("b (t p) d -> p (b t) d", p=P)
        out_rows = out.rearrange("b (t p) d -> p (b t) d", p=P)
        xs_rows = xs.rearrange("(n p) d -> p n d", p=P)
        ys_rows = ys.rearrange("(n p) d -> p n d", p=P)
        xs_zero = xs.rearrange("(p n) d -> p (n d)", p=P)
        ZW = NB * BLK * D // P

        x_loaded = [sem(f"x_loaded{c}") for c in range(NC)]
        cst_loaded, att_loaded, bt_loaded = sem("cst_loaded"), sem("att_loaded"), sem("bt_loaded")
        raw_loaded = [sem("raw_loaded0"), sem("raw_loaded1")]
        b_loaded = [sem("b_loaded0"), sem("b_loaded1")]
        w_hi = [sem("w1_hi"), sem("w2_hi")]
        w_lo = [sem("w1_lo"), sem("w2_lo")]
        xhi_ready, xlo_ready = sem("xhi_ready"), sem("xlo_ready")
        hhi_ready, hlo_ready, rank_read = sem("hhi_ready"), sem("hlo_ready"), sem("rank_read")
        xin_loaded = [sem("xin_loaded0"), sem("xin_loaded1")]
        y_stored = [sem("y_stored0"), sem("y_stored1")]
        zero_made, zero_filled = sem("zero_made"), sem("zero_filled")
        dve_step, pool_step = sem("dve_step"), sem("pool_step")
        var_ready, rstd_ready = sem("var_ready"), sem("rstd_ready")
        xn_ready, xnT_ps, xnT_ready = sem("xn_ready"), sem("xnT_ps"), sem("xnT_ready")
        fold_ps, fold_sb = sem("fold_ps"), sem("fold_sb")
        score_ps, bias_ready, prob_ready = sem("score_ps"), sem("bias_ready"), sem("prob_ready")
        pooled_div, pooledT_ps = sem("pooled_div"), sem("pooledT_ps")
        rsum_ready, probT_ps, probT_ready = sem("rsum_ready"), sem("probT_ps"), sem("probT_ready")
        pooled_ps, pooled_sb = sem("pooled_ps"), sem("pooled_sb")
        headed_ps, headed_sb = sem("headed_ps"), sem("headed_sb")
        mix_ready, m_ps, m_ready, cbc_ready = sem("mix_ready"), sem("m_ps"), sem("m_ready"), sem("cbc_ready")
        xc_ready, proj_ps, x1_ready = sem("xc_ready"), sem("proj_ps"), sem("x1_ready")
        var2_ready, zscale_ready = sem("var2_ready"), sem("zscale_ready")
        z_ready, zT_ps, zT_ready = sem("z_ready"), sem("zT_ps"), sem("zT_ready")
        logits_sb, lgT_ps = sem("logits_sb"), sem("lgT_ps")
        logits_ps, el_ready, onehot_ready = sem("logits_ps"), sem("el_ready"), sem("onehot_ready")
        rank_ps, routed = sem("rank_ps"), sem("routed")
        scattered = sem("scattered")
        up_ps, hid_ready, down_done, out_done = sem("up_ps"), sem("hid_ready"), sem("down_done"), sem("out_done")
        blkT_ps = sem("blkT_ps")
        bias_added, combined_half = sem("bias_added"), sem("combined_half")
        gathered = [sem(f"gathered{r}") for r in range(4)]
        combined, out_stored = sem("combined"), sem("out_stored")

        GS2 = SH + NB
        order = []
        for i in range(SH + 1):
            if i < SH:
                order += [(2 * i, 0), (2 * i + 1, 1)]
            if i >= 1:
                order += [(NT // B + 2 * i - 2, 2), (NT // B + 2 * i - 1, 3)]

        block = ctx.enter_context(nc.Block())

        @block.sync
        def _(sp):
            for c in range(NC):
                sp.dma_start(x_sb[:, c * CH:(c + 1) * CH, :],
                             x_rows[:, c * CH:(c + 1) * CH, :]).then_inc(x_loaded[c], 16)
            def matrix(u, h, e):
                if not (isinstance(u, int) and u == 0):
                    sp.wait_ge(w_lo[h], u)
                src = wpack[e] if isinstance(e, int) else wpack[bass.ds(e, 1)].rearrange("a p n -> (a p) n")
                sp.dma_start(raw[:, h, :], src[:, h * W2:(h + 1) * W2]).then_inc(raw_loaded[h], 16)

            def biases(us, e):
                if isinstance(e, int):
                    one, two = b1pack[e], b2pack[e:e + 1, :]
                else:
                    one, two = b1pack[bass.ds(e, 1)].rearrange("a p n -> (a p) n"), b2pack[bass.ds(e, 1), :]
                sp.dma_start(b1[:, us, :], one).then_inc(b_loaded[us], 16)
                sp.dma_start(b2[:, us, :], two.to_broadcast([P, D])).then_inc(b_loaded[us], 16)

            def shared_rows(g, gs, i):
                sp.dma_start(xin[:, gs, :, :], z_sb[:, bass.ds(2 * i, 2), :]).then_inc(xin_loaded[gs], 16)

            def block_rows(j, gs):
                sp.dma_start(xin[:, gs, :, :], xs_rows[:, bass.ds(2 * j, 2), :]).then_inc(xin_loaded[gs], 16)

            def store(j, s):
                sp.dma_start(ys_rows[:, bass.ds(2 * j, 2), :], yo[:, s, :, :]).then_inc(y_stored[s], 16)

            matrix(0, 0, E)
            matrix(0, 1, E)
            biases(0, E)
            sp.wait_ge(zero_made, 1)
            zeros = fold[:].rearrange("p a k b d -> p (a k b d)")
            done = 0
            while done < ZW:
                n = min(2 * KD * B * D, ZW - done)
                sp.dma_start(xs_zero[:, done:done + n], zeros[:, 0:n]).then_inc(zero_filled, 16)
                done += n
            sp.wait_ge(z_ready, NT)
            sp.wait_ge(lgT_ps, 2)
            shared_rows(0, 0, 0)
            shared_rows(1, 1, 1)
            for g in range(2, SH):
                if g == 3:
                    sp.wait_ge(routed, 1)
                    e = sp.value_load(eid[0:1, 0:1], min_val=0, max_val=E - 1)
                    matrix(1, 0, e)
                    matrix(1, 1, e)
                    biases(1, e)
                sp.wait_ge(blkT_ps, g - 1)
                shared_rows(g, g % 2, g)

            def prepare(j, s, turned=True):
                sp.wait_ge(blkT_ps, SH + j - 1)
                block_rows(j, s)
                if isinstance(j, int) and j == 0:
                    return
                e = sp.value_load(eid[0:1, bass.ds(j, 1)], min_val=0, max_val=E - 1)
                matrix(j + 1, 0, e)
                matrix(j + 1, 1, e)
                sp.wait_ge(out_done, SH + j - 1)
                if isinstance(j, int) and j == 1:
                    sp.wait_ge(bias_added, SH)
                biases(1 - s, e)
                if not (isinstance(j, int) and j < 2):
                    store(j - 2, s)

            sp.wait_ge(scattered, 16 * 2 * NT)
            for j in range(3):
                prepare(j, j % 2)
            with sp.Fori(0, (NB - 3) // 6) as i:
                for q in range(6):
                    prepare(6 * i + 3 + q, (3 + q) % 2)
            for i in range(SH):
                g = GS2 + i
                sp.wait_ge(blkT_ps, g - 1)
                shared_rows(g, g % 2, SH + i)
                if i == 0:
                    matrix(NB + 1, 0, E)
                    matrix(NB + 1, 1, E)
                if i < 2:
                    sp.wait_ge(out_done, g - 1)
                    if i == 0:
                        biases(0, E)
                    store(NB - 2 + i, (NB + i) % 2)

            def result(t, n):
                sp.wait_ge(combined, n)
                sp.dma_start(out_rows[:, bass.ds(t, 2), :], x_sb[:, bass.ds(t, 2), :]).then_inc(out_stored, 16)

            result(0, 2)
            with sp.Fori(1, SH) as i:
                result(2 * i, 4 * i)
                result(2 * i + NT // B - 2, 4 * i + 2)
            result(NT - 2, NT)
            sp.wait_ge(out_stored, 16 * 2 * SH)

        @block.gpsimd
        def _(pool):
            nc.gpsimd.memset(fold[:], 0.0).then_inc(zero_made, 1)
            count = [0]

            def link(ins):
                count[0] += 1
                ins.then_inc(pool_step, 1)
                pool.wait_ge(pool_step, count[0])

            half = cst[:, C_HALF:C_HALF + CH]
            pool.wait_ge(cst_loaded, 16)
            for c in range(NC):
                a, z = c * CH, (c + 1) * CH
                pool.wait_ge(var_ready, c + 1)
                nc.gpsimd.tensor_tensor(rstd[:, a:z], vare[:, a:z], half, ALU.pow).then_inc(rstd_ready, 1)
            pool.wait_ge(cbc_ready, 1)
            pool.wait_ge(xn_ready, NT)
            for c in range(NC + 1):
                if c < NC:
                    for t in range(c * CH, (c + 1) * CH):
                        nc.gpsimd.tensor_tensor(x_sb[:, t, :], x_sb[:, t, :], cbc[:, t // (NT // B), :],
                                                ALU.add).then_inc(xc_ready, 1)
                if c >= 1:
                    a, z = (c - 1) * CH, c * CH
                    pool.wait_ge(var2_ready, c)
                    link(nc.gpsimd.tensor_tensor(rr[:, a:z], vare[:, a:z], half, ALU.pow))
                    link(nc.gpsimd.tensor_tensor(rr2[:, a:z], rr[:, a:z], rr[:, a:z], ALU.mult))
                    link(nc.gpsimd.tensor_tensor(rr2[:, a:z], rr2[:, a:z], var[:, a:z], ALU.mult))
                    link(nc.gpsimd.tensor_scalar(rr2[:, a:z], rr2[:, a:z], EPS_RMS, None, ALU.add))
                    link(nc.gpsimd.tensor_tensor(rr3[:, a:z], rr2[:, a:z], half, ALU.pow))
                    nc.gpsimd.tensor_tensor(zscale[:, a:z], rr3[:, a:z], rr[:, a:z],
                                            ALU.mult).then_inc(zscale_ready, 1)
            pool.wait_ge(zero_filled, 16 * (-(-ZW // (2 * KD * B * D))))
            pool.wait_ge(routed, 1)
            for t in range(NT):
                for k in range(2):
                    nc.gpsimd.indirect_dma_start(
                        xs, bass.IndirectOffsetOnAxis(pos[:, k, t:t + 1], 0), z_sb[:, t, :], None
                    ).then_inc(scattered, 16)
            pool.wait_ge(y_stored[0], 16 * ((NB + 1) // 2))
            pool.wait_ge(y_stored[1], 16 * (NB // 2))
            for n, (t, q) in enumerate(order):
                before = [m for m in range(n) if order[m][1] == q]
                if before:
                    pool.wait_ge(combined, before[-1] + 1)
                for k in range(2):
                    nc.gpsimd.indirect_dma_start(
                        ring[:, q, k, :], None, ys, bass.IndirectOffsetOnAxis(pos[:, k, t:t + 1], 0)
                    ).then_inc(gathered[q], 16)

        @block.tensor
        def _(pe):
            mm = nc.tensor.matmul

            pe.wait_ge(att_loaded, 32)
            pe.wait_ge(cst_loaded, 16)
            for k in range(KD):
                for n in range(KD):
                    mm(psD[:, 1, 32 * k:32 * k + 32], wqT[:, n, k * P:(k + 1) * P], wqa[:, n, :],
                       start=(n == 0), stop=(n == KD - 1))
            for b in range(B):
                for n in range(KD):
                    last = mm(psD[32 * b:32 * b + 32, 1, 64:65], wqa[:, n, :], att[:, A_BQ + n:A_BQ + n + 1],
                              start=(n == 0), stop=(n == KD - 1))
            last.then_inc(fold_ps, 1)

            for q in range(NT // 2):
                pe.wait_ge(xn_ready, 2 * q + 2)
                if q >= 2:
                    pe.wait_ge(xnT_ready, q - 1)
                for tt in range(2):
                    for k in range(KD):
                        last = nc.tensor.transpose(psT[:, q % 2, k * 256 + tt * P:k * 256 + (tt + 1) * P],
                                                   z_sb[:, 2 * q + tt, k * P:(k + 1) * P], ident)
                last.then_inc(xnT_ps, 1)

            def scores(lhs):
                for g in range(4):
                    for b in range(B):
                        for k in range(KD):
                            last = mm(psU[32 * b:32 * b + 32, g, :], lhs(k, b),
                                      xT[:, k, b * S + g * 512:b * S + (g + 1) * 512],
                                      start=(k == 0), stop=(k == KD - 1))
                last.then_inc(score_ps, 1)

            def pool_tokens(r):
                pe.wait_ge(prob_ready, r + 1)
                for i in range(S // P):
                    last = nc.tensor.transpose(psT[:, i // 8, (i % 8) * 64:(i % 8 + 1) * 64],
                                               prob[:, i * P:(i + 1) * P], ident[0:64, 0:64])
                last.then_inc(probT_ps, 1)
                pe.wait_ge(probT_ready, r + 1)
                for b in range(B):
                    for i in range(S // P):
                        last = mm(psD[32 * b:32 * b + NH, 1, 128:128 + D], eT[:, i, b * NH:(b + 1) * NH],
                                  z_sb[:, b * (S // P) + i, :], start=(i == 0), stop=(i == S // P - 1))
                last.then_inc(pooled_ps, 1)
                pe.wait_ge(pooled_div, r + 1)
                for k in range(KD):
                    for b in range(B):
                        last = nc.tensor.transpose(psT[:, b, k * NH:(k + 1) * NH],
                                                   pooled[32 * b:32 * b + NH, k * P:(k + 1) * P],
                                                   ident[32 * b:32 * b + NH, 32 * b:32 * b + NH])
                last.then_inc(pooledT_ps, 1)
                pe.wait_ge(pooled_sb, r + 1)
                wmat = (wq, wk)[r]
                for n in range(KD):
                    for k in range(KD):
                        last = mm(psD[:, 1, 384 + 32 * n:416 + 32 * n], wmat[:, k, n * P:(n + 1) * P],
                                  pool_sb[:, k, :], start=(k == 0), stop=(k == KD - 1))
                last.then_inc(headed_ps, 1)

            pe.wait_ge(fold_sb, 1)
            pe.wait_ge(xnT_ready, NT // 2)
            scores(lambda k, b: aq[:, k, :])
            pool_tokens(0)

            pe.wait_ge(headed_sb, 1)
            for k in range(KD):
                for n in range(KD):
                    mm(psD[:, 1, 64 * k:64 * k + 64], wkT[:, n, k * P:(k + 1) * P],
                       gk[:, n, :, :].rearrange("p b h -> p (b h)"), start=(n == 0), stop=(n == KD - 1))
            for b in range(B):
                for n in range(KD):
                    last = mm(psD[32 * b:32 * b + 32, 1, 448:449], gk[:, n, b, :], att[:, A_BK + n:A_BK + n + 1],
                              start=(n == 0), stop=(n == KD - 1))
            last.then_inc(fold_ps, 1)
            pe.wait_ge(fold_sb, 2)
            scores(lambda k, b: bk_[:, k, 32 * b:32 * b + 32])
            pool_tokens(1)

            pe.wait_ge(mix_ready, 1)
            for b in range(B):
                for k in range(KD):
                    for n in range(KD):
                        mm(psT[:, b, k * D:(k + 1) * D], wqT[:, n, k * P:(k + 1) * P], gt[:, n, b, :],
                           start=(n == 0), stop=(n == KD - 1))
                for n in range(KD):
                    last = mm(psD[:, 1, b * D:(b + 1) * D], bqrep[:, n, :], gt[:, n, b, :],
                              start=(n == 0), stop=(n == KD - 1))
            last.then_inc(m_ps, 1)
            pe.wait_ge(m_ready, 1)

            def project(q):
                if q >= 4:
                    pe.wait_ge(x1_ready, q - 3)
                for tt in range(2):
                    t = 2 * q + tt
                    for k in range(KD):
                        last = mm(psU[:, q % 4, tt * D:(tt + 1) * D], xT[:, k, t * P:(t + 1) * P],
                                  mt[:, k, t // (NT // B), :], start=(k == 0), stop=(k == KD - 1))
                last.then_inc(proj_ps, 1)

            def turn_z(q):
                pe.wait_ge(z_ready, 2 * q + 2)
                if q >= 2:
                    pe.wait_ge(zT_ready, q - 1)
                for tt in range(2):
                    for k in range(KD):
                        last = nc.tensor.transpose(psT[:, q % 2, k * 256 + tt * P:k * 256 + (tt + 1) * P],
                                                   z_sb[:, 2 * q + tt, k * P:(k + 1) * P], ident)
                last.then_inc(zT_ps, 1)

            def router(g):
                pe.wait_ge(zT_ready, 2 * g + 2)
                o = 32 * (g % 4)
                for k in range(KD):
                    last = mm(psD[o:o + 32, g // 4, :], rwT[:, k, :], xT[:, k, g * 512:(g + 1) * 512],
                              start=(k == 0), stop=(k == KD - 1))
                if g % 4 == 3:
                    last.then_inc(logits_ps, 1)

            QC = CH // 2
            for c in range(NC + 1):
                if c < NC:
                    for q in range(c * QC, (c + 1) * QC):
                        project(q)
                if c >= 1:
                    for q in range((c - 1) * QC, c * QC):
                        turn_z(q)
                    if c == 1:
                        pe.wait_ge(cbc_ready, 1)
                    router(2 * c - 2)
                    router(2 * c - 1)
            for r in range(2):
                pe.wait_ge(logits_sb, r + 1)
                for i in range(4):
                    last = nc.tensor.transpose(psT[:, r, i * P:(i + 1) * P], lgT[:, r, i * P:(i + 1) * P], ident)
                last.then_inc(lgT_ps, 1)

            pe.wait_ge(onehot_ready, 1)
            ohf = oh[:].rearrange("p t e -> p (t e)")
            mm(psD[:, 1, 0:NT * E], tri, ohf, start=True, stop=True)
            mm(psD[:, 1, NT * E:2 * NT * E], ones, ohf, start=True, stop=True).then_inc(rank_ps, 1)

            def turn(g, gs, uses):
                pe.wait_ge(xin_loaded[gs], 16 * uses)
                for half in range(2):
                    for k in range(KD):
                        last = nc.tensor.transpose(psT[:, gs, k * BLK + half * P:k * BLK + (half + 1) * P],
                                                   xin[:, gs, half, k * P:(k + 1) * P], ident)
                last.then_inc(blkT_ps, 1)

            def up(g, gs, slot):
                pe.wait_ge(xlo_ready, g + 1)
                for m in range(MH):
                    for k in range(KD):
                        col = slice(k * H + m * P, k * H + (m + 1) * P)
                        dst = psU[:, m // 2, (m % 2) * BLK:(m % 2 + 1) * BLK]
                        mm(dst, whi[:, slot, col], xhi[:, gs, k, :], start=(k == 0), stop=False)
                        mm(dst, whi[:, slot, col], xlo[:, gs, k, :], start=False, stop=False)
                        last = mm(dst, wlo[:, slot, col], xhi[:, gs, k, :], start=False, stop=(k == KD - 1))
                    if m % 2:
                        last.then_inc(up_ps, 1)

            def down(g, gs, slot):
                if not (isinstance(g, int) and g < 2):
                    pe.wait_ge(out_done, g - 1)
                for half in range(2):
                    for c in range(MH):
                        if half == 0 and c % 2 == 0:
                            pe.wait_ge(hlo_ready, g * (MH // 2) + c // 2 + 1)
                        rows = slice(half * P, (half + 1) * P)
                        col = slice(c * D, (c + 1) * D)
                        dst = psD[:, gs, half * D:(half + 1) * D]
                        mm(dst, hhi[:, c, rows], whi[:, slot, col], start=(c == 0), stop=False)
                        mm(dst, hhi[:, c, rows], wlo[:, slot, col], start=False, stop=False)
                        last = mm(dst, hlo[:, c, rows], whi[:, slot, col], start=False, stop=(c == MH - 1))
                last.then_inc(down_done, 1)

            def tile(g, gs, u, um, uses=None, fresh=True):
                if uses is not None:
                    turn(g + 1, 1 - gs, uses)
                if fresh:
                    pe.wait_ge(w_lo[0], u + 1)
                up(g, gs, 2 * um % 3)
                if isinstance(g, int) and g == 1:
                    pe.wait_ge(rank_read, 1)
                if fresh:
                    pe.wait_ge(w_lo[1], u + 1)
                down(g, gs, (2 * um + 1) % 3)

            pe.wait_ge(el_ready, 2)
            turn(0, 0, 1)
            tile(0, 0, 0, 0, 1)
            tile(1, 1, 0, 0, 2, False)
            with pe.Fori(1, SH // 2) as i:
                tile(2 * i, 0, 0, 0, i + 1, False)
                tile(2 * i + 1, 1, 0, 0, i + 2, False)
            for j in range(3):
                g = SH + j
                tile(g, g % 2, j + 1, (j + 1) % 3, (g + 1) // 2 + 1)
            with pe.Fori(0, (NB - 3) // 6) as i:
                for q in range(6):
                    tile(6 * i + SH + 3 + q, (SH + 3 + q) % 2, 6 * i + 4 + q, (4 + q) % 3,
                         3 * i + (SH + 4 + q) // 2 + 1)
            for i in range(SH):
                g = GS2 + i
                tile(g, g % 2, NB + 1, (NB + 1) % 3, (g + 1) // 2 + 1 if i < SH - 1 else None, i == 0)

        @block.scalar
        def _(act):
            act.dma_start(att[:, :], attn).then_inc(att_loaded, 16)
            act.dma_start(nw[:, :], norm).then_inc(att_loaded, 16)
            act.dma_start(cst[:, :], consts).then_inc(cst_loaded, 16)
            act.dma_start(bt_bc[:, :], bt.to_broadcast([P, D])).then_inc(bt_loaded, 16)
            copy = ACT.Copy
            for q in range(NT // 2):
                act.wait_ge(xnT_ps, q + 1)
                nc.scalar.activation(xT[:, :, q * 256:(q + 1) * 256],
                                     psT[:, q % 2, :].rearrange("p (k n) -> p k n", k=KD), copy).then_inc(xnT_ready, 1)

            def split_hi(h, u, slot):
                act.wait_ge(raw_loaded[h], 16 * (u + 1))
                nc.scalar.activation(whi[:, slot, :], raw[:, h, :], copy).then_inc(w_hi[h], 1)

            split_hi(0, 0, 0)
            split_hi(1, 0, 1)
            for r in range(2):
                act.wait_ge(bias_ready, r + 1)
                act.wait_ge(zero_filled, 16 * (-(-ZW // (2 * KD * B * D))))
                nc.scalar.activation(prob[:, :], psU[0:64, :, :].rearrange("p g n -> p (g n)"), ACT.Exp,
                                     bias=small[:, 4:5], scale=SCALE,
                                     accum_out=small[:, 5:6]).then_inc(prob_ready, 1)
                act.wait_ge(probT_ps, r + 1)
                nc.scalar.activation(
                    eT[:].rearrange("p i (b h) -> p i b h", b=B),
                    psT[:].rearrange("p a (i b h) -> p (a i) b h", b=B, h=32)[:, :, :, 0:NH], copy).then_inc(probT_ready, 1)
                act.wait_ge(pooled_ps, r + 1)
                act.wait_ge(rsum_ready, r + 1)
                for b in range(B):
                    own = slice(32 * b, 32 * b + NH)
                    last = nc.scalar.activation(pooled[own, :], psD[own, 1, 128:128 + D], copy, scale=small[own, 6:7])
                last.then_inc(pooled_div, 1)
                act.wait_ge(pooledT_ps, r + 1)
                nc.scalar.activation(pool_sb[:].rearrange("p k (b h) -> p k b h", b=B),
                                     psT[:, :, 0:KD * NH].rearrange("p b (k h) -> p k b h", k=KD), copy).then_inc(pooled_sb, 1)
            act.wait_ge(m_ps, 1)
            for b in range(B):
                last = nc.scalar.activation(mt[:, :, b, :], psT[:, b, :].rearrange("p (k n) -> p k n", k=KD), copy)
            last.then_inc(m_ready, 1)
            for q in range(NT // 2):
                act.wait_ge(zT_ps, q + 1)
                for k in range(KD):
                    last = nc.scalar.activation(xT[:, k, q * 256:(q + 1) * 256], psT[:, q % 2, k * 256:(k + 1) * 256],
                                                copy, scale=nw[:, k:k + 1])
                last.then_inc(zT_ready, 1)
                if q % 8 == 7 and q > 8 or q == 11:
                    r = q // 8 if q % 8 == 7 else 0
                    act.wait_ge(logits_ps, r + 1)
                    nc.scalar.activation(lgT[:, r, :], psD[:, r, :], copy).then_inc(logits_sb, 1)
            for r in range(2):
                act.wait_ge(lgT_ps, r + 1)
                nc.scalar.activation(
                    pr[:, r * 16:(r + 1) * 16, :].rearrange("p (g i) e -> p i g e", g=4),
                    psT[:, r, :].rearrange("p (i g e) -> p i g e", i=4, g=4)[:, :, :, 0:E],
                    ACT.Exp, scale=-1.0).then_inc(el_ready, 1)

            def turned_hi(g, gs):
                act.wait_ge(blkT_ps, g + 1)
                for k in range(KD):
                    last = nc.scalar.activation(xhi[:, gs, k, :], psT[:, gs, k * BLK:(k + 1) * BLK], copy,
                                                scale=nw[:, k:k + 1])
                last.then_inc(xhi_ready, 1)

            def tile(g, gs, us, loads, turn=True, fresh=None):
                if turn:
                    turned_hi(g + 1, 1 - gs)
                act.wait_ge(b_loaded[us], 32 * loads)
                for m in range(MH):
                    if m % 2 == 0:
                        act.wait_ge(up_ps, g * (MH // 2) + m // 2 + 1)
                    last = nc.scalar.activation(hid[:, m, :], psU[:, m // 2, (m % 2) * BLK:(m % 2 + 1) * BLK],
                                                ACT.Relu, bias=b1[:, us, m:m + 1])
                    if m % 2:
                        last.then_inc(hid_ready, 1)
                if fresh is not None:
                    u, um = fresh
                    act.wait_ge(down_done, g)
                    split_hi(0, u, 2 * um % 3)
                    split_hi(1, u, (2 * um + 1) % 3)

            turned_hi(0, 0)
            tile(0, 0, 0, 1)
            with act.Fori(0, SH // 2 - 1) as i:
                tile(2 * i + 1, 1, 0, 1)
                tile(2 * i + 2, 0, 0, 1)
            tile(SH - 1, 1, 0, 1, fresh=(1, 1))
            for j in range(3):
                g, u = SH + j, j + 1
                tile(g, g % 2, u % 2, u // 2 + 1, fresh=(u + 1, (u + 1) % 3))
            with act.Fori(0, (NB - 3) // 6) as i:
                for q in range(6):
                    tile(6 * i + SH + 3 + q, (SH + 3 + q) % 2, (4 + q) % 2, 3 * i + (4 + q) // 2 + 1,
                         fresh=(6 * i + 5 + q, (5 + q) % 3))
            for i in range(SH):
                g = GS2 + i
                tile(g, g % 2, (NB + 1) % 2, (NB + 1) // 2 + 1, i < SH - 1)

        @block.vector
        def _(dve):
            count = [0]

            def link(ins):
                count[0] += 1
                ins.then_inc(dve_step, 1)
                dve.wait_ge(dve_step, count[0])

            V = nc.vector

            def moments(c, eps, ready):
                a, z = c * CH, (c + 1) * CH
                st = stats[:, a:z, :]
                V.tensor_tensor(ssum[:, a:z], st[:, :, 1], st[:, :, 4], ALU.add)
                V.tensor_tensor(sm2[:, a:z], st[:, :, 2], st[:, :, 5], ALU.add)
                link(V.tensor_tensor(sdif[:, a:z], st[:, :, 1], st[:, :, 4], ALU.subtract))
                V.tensor_scalar(mean[:, a:z], ssum[:, a:z], 0.5, None, ALU.mult)
                V.tensor_scalar(sm2[:, a:z], sm2[:, a:z], 1.0 / D, None, ALU.mult)
                link(V.scalar_tensor_tensor(sdif[:, a:z], sdif[:, a:z], 0.25, sdif[:, a:z], ALU.mult, ALU.mult))
                link(V.tensor_tensor(var[:, a:z], sdif[:, a:z], sm2[:, a:z], ALU.add))
                V.tensor_scalar(vare[:, a:z], var[:, a:z], eps, None, ALU.add).then_inc(ready, 1)

            def normalise(c):
                dve.wait_ge(rstd_ready, c + 1)
                for t in range(c * CH, (c + 1) * CH):
                    V.tensor_scalar(z_sb[:, t, :], x_sb[:, t, :], mean[:, t:t + 1], rstd[:, t:t + 1],
                                    ALU.subtract, ALU.mult).then_inc(xn_ready, 1)

            for c in range(NC):
                dve.wait_ge(x_loaded[c], 16)
                for t in range(c * CH, (c + 1) * CH):
                    last = V.bn_stats(stats[:, t, :], x_sb[:, t, :])
                link(last)
                moments(c, EPS_LN, var_ready)
                if c >= 1:
                    normalise(c - 1)
            dve.wait_ge(fold_ps, 1)
            V.tensor_copy(aq[:].rearrange("p k h -> p (k h)"), psD[:, 1, 0:64])
            V.tensor_tensor(small[:, 0:1], psD[0:64, 1, 64:65], att[0:64, A_BQA:A_BQA + 1],
                            ALU.add).then_inc(fold_sb, 1)
            normalise(NC - 1)
            dve.wait_ge(bt_loaded, 16)


            def split_lo(h, u, slot):
                dve.wait_ge(w_hi[h], u + 1)
                V.tensor_tensor(wlo[:, slot, :], raw[:, h, :], whi[:, slot, :].bitcast(F32),
                                ALU.subtract).then_inc(w_lo[h], 1)

            split_lo(0, 0, 0)
            split_lo(1, 0, 1)
            for n in range(KD):
                V.tensor_scalar(bqrep[:, n, :], ones, att[:, A_BQ + n:A_BQ + n + 1], None, ALU.mult)

            def softmax(r):
                dve.wait_ge(score_ps, r + 1)
                link(V.tensor_reduce(small[:, 1:2], psU[0:64, :, :].rearrange("p g n -> p (g n)"), X, ALU.max))
                link(V.tensor_tensor(small[:, 2:3], small[:, 1:2], small[:, 0:1], ALU.add))
                link(V.tensor_tensor(small[:, 3:4], small[:, 0:1], small[:, 2:3], ALU.subtract))
                V.tensor_scalar(small[:, 4:5], small[:, 3:4], SCALE, None, ALU.mult).then_inc(bias_ready, 1)
                dve.wait_ge(prob_ready, r + 1)
                V.reciprocal(small[:, 6:7], small[:, 5:6]).then_inc(rsum_ready, 1)

            def heads(r):
                dve.wait_ge(headed_ps, r + 1)
                for n in range(KD):
                    src = psD[:, 1, 384 + 32 * n:416 + 32 * n].rearrange("p (b h) -> p b h", b=B)
                    last = V.tensor_tensor(dtmp[:, n, :, :], src, hm[:, n:n + 1, :].to_broadcast([P, B, NH]), ALU.mult)
                link(last)
                link(V.tensor_reduce(dred[:], dtmp[:], X, ALU.add))

            softmax(0)
            heads(0)
            for n in range(KD):
                last = V.tensor_scalar(pq[:, n, :], dred[:, n, :], att[:, A_BQ + n:A_BQ + n + 1], None, ALU.add)
            link(last)
            for n in range(KD):
                for b in range(B):
                    last = V.tensor_scalar(gk[:, n, b, :], wka[:, n, :], pq[:, n, b:b + 1], None, ALU.mult)
            last.then_inc(headed_sb, 1)
            dve.wait_ge(fold_ps, 2)
            V.tensor_copy(bk_[:].rearrange("p k h -> p (k h)"), psD[:, 1, 0:128])
            V.tensor_tensor(small[:, 0:1], psD[0:64, 1, 448:449], att[0:64, A_BKA:A_BKA + 1],
                            ALU.add).then_inc(fold_sb, 1)
            dve.wait_ge(fold_sb, 2)
            softmax(1)
            heads(1)
            for n in range(KD):
                last = V.tensor_scalar(dred[:, n, :], dred[:, n, :], att[:, A_BK + n:A_BK + n + 1], None, ALU.add)
            link(last)
            link(V.tensor_tensor(pk[:], dred[:], pq[:], ALU.mult))
            dve.wait_ge(zero_filled, 16 * (-(-ZW // (2 * KD * B * D))))
            for n in range(KD):
                for b in range(B):
                    last = V.scalar_tensor_tensor(gt[:, n, b, :], wt[:, n, :], pk[:, n, b:b + 1], eye[:, n, :],
                                                  ALU.mult, ALU.add)
            last.then_inc(mix_ready, 1)
            dve.wait_ge(m_ps, 1)
            for b in range(B):
                last = V.tensor_tensor(cbc[:, b, :], psD[:, 1, b * D:(b + 1) * D], bt_bc[:, :], ALU.add)
            last.then_inc(cbc_ready, 1)

            QC = CH // 2
            for c in range(NC + 1):
                if c < NC:
                    for q in range(c * QC, (c + 1) * QC):
                        dve.wait_ge(proj_ps, q + 1)
                        dve.wait_ge(xc_ready, 2 * q + 2)
                        pair = x_sb[:, 2 * q:2 * q + 2, :]
                        V.tensor_tensor(pair, psU[:, q % 4, :].rearrange("p (t n) -> p t n", t=2), pair,
                                        ALU.add).then_inc(x1_ready, 1)
                        dve.wait_ge(x1_ready, q + 1)
                        for t in (2 * q, 2 * q + 1):
                            last = V.bn_stats(stats[:, t, :], x_sb[:, t, :])
                    link(last)
                    moments(c, EPS_LN, var2_ready)
                if c >= 1:
                    dve.wait_ge(zscale_ready, c)
                    for t in range((c - 1) * CH, c * CH):
                        V.tensor_scalar(z_sb[:, t, :], x_sb[:, t, :], mean[:, t:t + 1], zscale[:, t:t + 1],
                                        ALU.subtract, ALU.mult).then_inc(z_ready, 1)

            def over_e(ap):
                return ap.rearrange("p (t o) -> p t o", o=1).to_broadcast([P, NT, E])

            def line(tensor):
                return tensor[:].rearrange("p t e -> p (t e)")

            dve.wait_ge(el_ready, 2)
            link(V.tensor_scalar(line(pr), line(pr), 1.0, None, ALU.add))
            link(V.reciprocal(line(pr), line(pr)))

            def best(src, row, onehot):
                link(V.tensor_reduce(top[:, row, :], src[:], X, ALU.max))
                link(V.tensor_tensor(ra[:], src[:], over_e(top[:, row, :]), ALU.is_equal))
                link(V.scalar_tensor_tensor(line(ra), line(ra), -float(E), iota.rearrange("p t e -> p (t e)"),
                                            ALU.mult, ALU.add))
                link(V.tensor_reduce(top[:, row + 1, :], ra[:], X, ALU.min))
                link(V.tensor_scalar(top[:, row + 1, :], top[:, row + 1, :], float(E), None, ALU.add))
                link(V.tensor_tensor(onehot[:], iota, over_e(top[:, row + 1, :]), ALU.is_equal))

            best(pr, 0, oh1)
            link(V.scalar_tensor_tensor(line(pr2), line(oh1), -2.0, line(pr), ALU.mult, ALU.add))
            best(pr2, 2, oh2)
            V.tensor_tensor(line(oh), line(oh1), line(oh2), ALU.add).then_inc(onehot_ready, 1)
            link(V.tensor_tensor(top[:, 4, :], top[:, 0, :], top[:, 2, :], ALU.add))
            link(V.tensor_scalar(top[:, 4, :], top[:, 4, :], EPS_W, None, ALU.add))
            link(V.reciprocal(top[:, 5, :], top[:, 4, :]))
            V.tensor_tensor(top[:, 6, :], top[:, 0, :], top[:, 5, :], ALU.mult)
            link(V.tensor_tensor(top[:, 7, :], top[:, 2, :], top[:, 5, :], ALU.mult))
            dve.wait_ge(rank_ps, 1)
            link(V.tensor_copy(tot[:], psD[:, 1, NT * E:2 * NT * E].rearrange("p (t e) -> p e t", e=E)))
            link(V.tensor_tensor_scan(inc[:].rearrange("p e t -> p (e t)"), cst[:, C_SCAN:C_SCAN + E * NT],
                                      tot[:].rearrange("p e t -> p (e t)"), 0.0, ALU.mult, ALU.add))
            link(V.tensor_tensor(thr[:], inc[:, :, NT - 1:NT].to_broadcast([P, E, MAXT]),
                                 cst[:, C_THR:C_THR + E * MAXT].rearrange("p (e m) -> p e m", e=E), ALU.is_gt))
            link(V.tensor_reduce(blk[:, 0, :], thr[:], X, ALU.add))
            link(V.tensor_tensor_scan(blk[:, 1, :], ones[:, 0:E], blk[:, 0, :], 0.0, ALU.mult, ALU.add))
            link(V.tensor_tensor(blk[:, 2, :], blk[:, 1, :], blk[:, 0, :], ALU.subtract))
            link(V.tensor_scalar(blk[:, 3, :], blk[:, 2, :], float(BLK), None, ALU.mult))
            link(V.tensor_tensor(posm[:], inc[:], tot[:], ALU.subtract))
            V.tensor_tensor(posm[:], posm[:], psD[:, 1, 0:NT * E].rearrange("p (t e) -> p e t", e=E),
                            ALU.add).then_inc(rank_read, 1)
            dve.wait_ge(rank_read, 1)
            link(V.tensor_tensor(posm[:], posm[:],
                                 blk[:, 3, :].rearrange("p (e o) -> p e o", o=1).to_broadcast([P, E, NT]), ALU.add))
            for k, (onehot, prod) in enumerate(((oh1, ra), (oh2, pr2))):
                link(V.tensor_tensor(prod[:], onehot[:], posm[:].rearrange("p e t -> p t e"), ALU.mult))
                link(V.tensor_reduce(top[:, 4 + k, :], prod[:], X, ALU.add))
                V.tensor_copy(pos[:, k, :], top[:, 4 + k, :])
            link(V.tensor_tensor(bcmp[:], cst[:, C_BLK:C_BLK + NBP * E].rearrange("p (n e) -> p n e", e=E),
                                 blk[:, 1:2, :].to_broadcast([P, NBP, E]), ALU.is_ge))
            link(V.tensor_reduce(eidf[:], bcmp[:], X, ALU.add))
            link(V.tensor_scalar(eidf[:], eidf[:], float(E - 1), None, ALU.min))
            V.tensor_copy(eid[:], eidf[:]).then_inc(routed, 1)

            def turned_lo(g, gs):
                dve.wait_ge(xhi_ready, g + 1)
                for k in range(KD):
                    last = V.scalar_tensor_tensor(xlo[:, gs, k, :], psT[:, gs, k * BLK:(k + 1) * BLK],
                                                  nw[:, k:k + 1], xhi[:, gs, k, :].bitcast(F32),
                                                  ALU.mult, ALU.subtract)
                last.then_inc(xlo_ready, 1)

            def hidden(g):
                for b in range(MH // 2):
                    two = slice(2 * b, 2 * b + 2)
                    n = g * (MH // 2) + b + 1
                    dve.wait_ge(hid_ready, n)
                    V.tensor_copy(hhi[:, two, :], hid[:, two, :]).then_inc(hhi_ready, 1)
                    dve.wait_ge(hhi_ready, n)
                    V.tensor_tensor(hlo[:, two, :], hid[:, two, :], hhi[:, two, :].bitcast(F32),
                                    ALU.subtract).then_inc(hlo_ready, 1)

            def shared_out(g, gs, t):
                dve.wait_ge(down_done, g + 1)
                pair = x_sb[:, bass.ds(t, 2), :]
                V.tensor_tensor(pair, psD[:, gs, :].rearrange("p (t n) -> p t n", t=2), pair,
                                ALU.add).then_inc(out_done, 1)
                dve.wait_ge(out_done, g + 1)
                return V.tensor_tensor(pair, pair, b2[:, 0:1, :].to_broadcast([P, 2, D]), ALU.add)

            def expert_out(j, s, stored, loads):
                dve.wait_ge(down_done, SH + j + 1)
                if stored is not None:
                    dve.wait_ge(y_stored[s], 16 * stored)
                dve.wait_ge(b_loaded[1 - s], 32 * loads)
                V.tensor_tensor(yo[:, s, :, :], psD[:, s, :].rearrange("p (t n) -> p t n", t=2),
                                b2[:, 1 - s:2 - s, :].to_broadcast([P, 2, D]), ALU.add).then_inc(out_done, 1)

            def fresh(u, um):
                split_lo(0, u, 2 * um % 3)
                split_lo(1, u, (2 * um + 1) % 3)

            turned_lo(0, 0)
            turned_lo(1, 1)
            hidden(0)
            with dve.Fori(1, SH // 2) as i:
                shared_out(2 * i - 2, 0, 4 * i - 4).then_inc(bias_added, 1)
                turned_lo(2 * i, 0)
                hidden(2 * i - 1)
                shared_out(2 * i - 1, 1, 4 * i - 2).then_inc(bias_added, 1)
                turned_lo(2 * i + 1, 1)
                hidden(2 * i)
            shared_out(SH - 2, 0, 2 * (SH - 2)).then_inc(bias_added, 1)
            turned_lo(SH, 0)
            hidden(SH - 1)
            fresh(1, 1)
            for j in range(3):
                g, u = SH + j, j + 1
                if j == 0:
                    shared_out(g - 1, (g - 1) % 2, 2 * (g - 1)).then_inc(bias_added, 1)
                else:
                    expert_out(j - 1, (j - 1) % 2, None, (u - 1) // 2 + 1)
                turned_lo(g + 1, (g + 1) % 2)
                hidden(g)
                fresh(u + 1, (u + 1) % 3)
            with dve.Fori(0, (NB - 3) // 6) as i:
                for q in range(6):
                    expert_out(6 * i + 2 + q, q % 2, 3 * i + (2 + q) // 2, 3 * i + (3 + q) // 2 + 1)
                    turned_lo(6 * i + SH + 4 + q, (SH + 4 + q) % 2)
                    hidden(6 * i + SH + 3 + q)
                    fresh(6 * i + 5 + q, (5 + q) % 3)

            def combine(n):
                t, q = order[n]
                uses = sum(1 for m in range(n + 1) if order[m][1] == q)
                dve.wait_ge(gathered[q], 32 * uses)
                V.scalar_tensor_tensor(x_sb[:, t, :], ring[:, q, 0, :], top[:, 6, t:t + 1], x_sb[:, t, :],
                                       ALU.mult, ALU.add).then_inc(combined_half, 1)
                dve.wait_ge(combined_half, n + 1)
                V.scalar_tensor_tensor(x_sb[:, t, :], ring[:, q, 1, :], top[:, 7, t:t + 1], x_sb[:, t, :],
                                       ALU.mult, ALU.add).then_inc(combined, 1)

            n = 0
            for i in range(SH + 1):
                g = GS2 + i
                if i == 0:
                    expert_out(NB - 1, (NB - 1) % 2, (NB - 1) // 2, NB // 2 + 1)
                else:
                    link(shared_out(g - 1, (g - 1) % 2, NT // B + 2 * (i - 1)))
                if i < SH - 1:
                    turned_lo(g + 1, (g + 1) % 2)
                if i < SH:
                    hidden(g)
                for _ in range(2 if i in (0, SH) else 4):
                    combine(n)
                    n += 1


def constants():
    c = np.zeros((P, C_ALL), np.float32)
    p = np.arange(P)
    c[:, C_ID:C_ID + P] = np.eye(P)
    c[:, C_TRI:C_TRI + P] = p[:, None] < p[None, :]
    c[:, C_ONE:C_ONE + P] = 1
    c[:, C_EYE:C_EYE + KD * D] = np.eye(D).reshape(KD, P, D).transpose(1, 0, 2).reshape(P, KD * D)
    feature = np.arange(KD)[None, :, None] * P + p[:, None, None]
    c[:, C_HM:C_HM + KD * NH] = (feature // (D // NH) == np.arange(NH)).reshape(P, KD * NH)
    c[:, C_IOTA:C_IOTA + NT * E] = np.tile(np.arange(E), NT)
    c[:, C_SCAN:C_SCAN + E * NT] = np.tile(np.arange(NT) > 0, E)
    c[:, C_THR:C_THR + E * MAXT] = np.tile(np.arange(MAXT) * BLK, E)
    c[:, C_BLK:C_BLK + NBP * E] = np.repeat(np.arange(NBP), E)
    c[:, C_HALF:C_HALF + NT] = -0.5
    return c


def rows_first(m):
    return np.ascontiguousarray(m.reshape(KD, P, -1).transpose(1, 0, 2).reshape(P, -1))


def kernel(**inputs):
    import concourse.bacc as bacc
    from concourse.bass_utils import run_bass_kernel_spmd

    a = {k: np.asarray(v) for k, v in inputs.items()}
    A, F = "L0_attn_", "L0_ffn_"
    heads = lambda m: np.concatenate([m, np.zeros((D, 32 - NH), np.float32)], 1)
    head_bias = lambda v: np.concatenate([v, np.zeros(16, np.float32)] * 2 + [np.zeros(64, np.float32)])[:, None]
    attn = np.concatenate([
        rows_first(a[A + "Wq"]), rows_first(a[A + "Wk"]), rows_first(a[A + "Wt"]),
        rows_first(a[A + "Wq"].T), rows_first(a[A + "Wk"].T),
        rows_first(heads(a[A + "Wqa"])), rows_first(heads(a[A + "Wka"])),
        rows_first(a[A + "bq"]), rows_first(a[A + "bk"]),
        rows_first(np.concatenate([a[F + "router_w"].T, np.zeros((D, 32 - E), np.float32)], 1)), head_bias(a[A + "bqa"]), head_bias(a[A + "bka"])], 1)
    w1 = np.concatenate([a[F + "ew1"], a[F + "sw1"][None]])
    w2 = np.concatenate([a[F + "ew2"], a[F + "sw2"][None]])
    w1 = w1.reshape(E + 1, KD, P, H).transpose(0, 2, 1, 3).reshape(E + 1, P, W2)
    w2 = w2.reshape(E + 1, MH, P, D).transpose(0, 2, 1, 3).reshape(E + 1, P, W2)
    arrays = {
        "x": a[A + "hidden_states"],
        "consts": constants(),
        "attn": attn,
        "norm": rows_first(a[F + "norm_weight"]),
        "bt": a[A + "bt"][None],
        "wpack": np.concatenate([w1, w2], 2),
        "b1pack": np.concatenate([a[F + "eb1"], a[F + "sb1"][None]]).reshape(E + 1, MH, P).transpose(0, 2, 1),
        "b2pack": np.concatenate([a[F + "eb2"], a[F + "sb2"][None]]),
    }
    nc = bacc.Bacc("TRN2", target_bir_lowering=False, num_devices=1)
    feeds, args = {}, []
    for name, v in arrays.items():
        v = np.ascontiguousarray(v)
        feeds["in_" + name] = v
        args.append(nc.dram_tensor("in_" + name, v.shape, mybir.dt.from_np(v.dtype), kind="ExternalInput").ap())
    out = nc.dram_tensor("out", (B, S, D), F32, kind="ExternalOutput").ap()
    build(nc, *args, out)
    return run_bass_kernel_spmd(nc, [feeds], core_ids=[0]).results[0]["out"]
```

```python
from contextlib import ExitStack

import numpy as np

import concourse.bass as bass
from concourse import mybir

ALU = mybir.AluOpType
ACT = mybir.ActivationFunctionType
F32 = mybir.dt.float32
F32R = mybir.dt.float32r
I32 = mybir.dt.int32
U32 = mybir.dt.uint32
X = mybir.AxisListType.X

P = 128
D, KD = 256, 2
H, MH = 1024, 8
E = 8
NH = 16
B, S = 2, 2048
T = B * S
NT = T // P
CH = 4
NC = NT // CH
BLK = 256
NB = (2 * T - E) // BLK + E
NBP = NB + 1
SH = B * S // BLK
SA = 9
SZ = SH - SA
W2 = KD * H
WROW = 2 * W2
EPS_LN, EPS_RMS, EPS_W = 1e-5, 1e-8, 1e-6
SCALE = float(D // NH) ** -0.5
MAXT = S * B // BLK

C_ID, C_TRI, C_ONE = 0, P, 2 * P
C_EYE = 3 * P
C_HM = C_EYE + KD * D
C_IOTA = C_HM + KD * NH
C_SCAN = C_IOTA + NT * E
C_THR = C_SCAN + E * NT
C_BLK = C_THR + E * MAXT
C_HILO = C_BLK + NBP * E
C_ALL = C_HILO + 1
A_WQ, A_WK, A_WT = 0, KD * D, 2 * KD * D
A_WQT, A_WKT = 3 * KD * D, 4 * KD * D
A_WQA = 5 * KD * D
A_WKA = A_WQA + KD * 32
A_BQ = A_WKA + KD * 32
A_BK = A_BQ + KD
A_RW = A_BK + KD
A_BQA = A_RW + KD * 32
A_BKA = A_BQA + 1
A_ALL = A_BKA + 1


def build(nc, x, consts, attn, norm, bt, wpack, b1pack, b2pack, out):
    with ExitStack() as ctx:
        def sb(name, shape, dt=F32):
            return ctx.enter_context(nc.sbuf_tensor(name, shape, dt))

        def ps(name, shape):
            return ctx.enter_context(nc.psum_tensor(name, shape, F32))

        def sem(name):
            return ctx.enter_context(nc.semaphore(name))

        xs = nc.dram_tensor("expert_in", [NB * BLK, D], F32).ap()
        ys = nc.dram_tensor("expert_out", [NB * BLK, D], F32).ap()

        x_sb = sb("x_sb", [P, NT, D])
        z_sb = sb("z_sb", [P, NT, D])
        cst = sb("cst", [P, C_ALL])
        nw = sb("nw", [P, KD])
        zero = sb("zero", [P, D])
        bt_bc = sb("bt_bc", [P, D])
        cpair = sb("cpair", [2, B, D], F32R)
        one2 = sb("one2", [2, P], F32R)
        bqrep = sb("bqrep", [P, KD, 32])
        stats = sb("stats", [P, NT, 6])
        ssum = sb("ssum", [P, NT])
        sdif = sb("sdif", [P, NT])
        sm2 = sb("sm2", [P, NT])
        mean = sb("mean", [P, NT])
        var = sb("var", [P, NT])
        vare = sb("vare", [P, NT])
        rstd = sb("rstd", [P, NT])
        nmr = sb("nmr", [P, NT])
        half = sb("half", [P, CH])
        zscale = sb("zscale", [P, NT])
        aq = sb("aq", [P, KD, 32])
        bk_ = sb("bk_", [P, B, KD, 32])
        gk = sb("gk", [P, KD, B, 32])
        pool_sb = sb("pool_sb", [P, B, KD, NH])
        dtmp = sb("dtmp", [P, B, KD, NH])
        dred = sb("dred", [P, B, KD])
        pq = sb("pq", [P, B, KD])
        pk = sb("pk", [P, B, KD])
        small = sb("small", [P, B, 8])
        mrow = sb("mrow", [1, B, 32])
        pooled = sb("pooled", [P, B, D])
        top = sb("top", [P, 8, NT])
        posm = sb("posm", [P, E, NT])
        sel = posm[:].rearrange("p e t -> p (e t)")[:, 0:P]
        own = posm[:].rearrange("p e t -> p (e t)")[:, P:P + 32]
        blk = sb("blk", [P, 4, E])
        thr = sb("thr", [P, E, MAXT])
        bcmp = sb("bcmp", [P, NBP, E])
        eidf = sb("eidf", [P, NBP])
        eid = sb("eid", [P, NBP], I32)
        pos = sb("pos", [P, 2, NT], U32)
        raw = sb("raw", [P, 2, W2])
        whi = sb("whi", [P, 3, W2], F32R)
        wlo = sb("wlo", [P, 3, W2], F32R)
        b1 = sb("b1", [P, 2, MH])
        b2 = sb("b2", [P, 2, D])
        xin = sb("xin", [P, 2, 2, D])
        fold = sb("fold", [P, 2, B, KD, D])
        gt, mt = fold[:, 0], fold[:, 1]
        flat = fold[:].rearrange("p a b k d -> p (a b k d)")
        prob = flat[:, 0:B * 512].rearrange("p (b n) -> p b n", b=B)
        route = flat.rearrange("p (r n) -> p r n", r=8)
        pr, pr2, ra, oh1, oh2, oh = (route[:, i, :].rearrange("p (t e) -> p t e", e=E) for i in range(6))
        tot, inc = (route[:, i, :].rearrange("p (e t) -> p e t", e=E) for i in (6, 7))
        with ExitStack() as early:
            xT = early.enter_context(nc.sbuf_tensor("xT", [P, KD, T], F32))
            att = early.enter_context(nc.sbuf_tensor("att", [P, A_ALL], F32))
        xhi = sb("xhi", [P, 2, KD, BLK], F32R)
        xlo = sb("xlo", [P, 2, KD, BLK], F32R)
        hid = sb("hid", [P, MH, BLK])
        hhi = sb("hhi", [P, MH, BLK], F32R)
        hlo = sb("hlo", [P, MH, BLK], F32R)
        yo = sb("yo", [P, 2, 2, D])
        RING = 8
        ring = z_sb[:, 0:2 * RING, :].rearrange("p (q k) d -> p q k d", k=2)

        psT = ps("psT", [P, 2, 512])
        psU = ps("psU", [P, 4, 512])
        psD = ps("psD", [P, 2, 512])

        ident = cst[:, C_ID:C_ID + P]
        tri = cst[:, C_TRI:C_TRI + P]
        ones = cst[:, C_ONE:C_ONE + P]
        iota = cst[:, C_IOTA:C_IOTA + NT * E].rearrange("p (t e) -> p t e", e=E)
        wq = att[:, A_WQ:A_WQ + KD * D].rearrange("p (k n) -> p k n", k=KD)
        wk = att[:, A_WK:A_WK + KD * D].rearrange("p (k n) -> p k n", k=KD)
        wt = att[:, A_WT:A_WT + KD * D].rearrange("p (k n) -> p k n", k=KD)
        wqT = att[:, A_WQT:A_WQT + KD * D].rearrange("p (k n) -> p k n", k=KD)
        wkT = att[:, A_WKT:A_WKT + KD * D].rearrange("p (k n) -> p k n", k=KD)
        wqa = att[:, A_WQA:A_WQA + KD * 32].rearrange("p (k n) -> p k n", k=KD)
        wka = att[:, A_WKA:A_WKA + KD * 32].rearrange("p (k n) -> p k n", k=KD)
        rwT = att[:, A_RW:A_RW + KD * 32].rearrange("p (k n) -> p k n", k=KD)
        hm = cst[:, C_HM:C_HM + KD * NH].rearrange("p (k h) -> p k h", k=KD)
        eye = cst[:, C_EYE:C_EYE + KD * D].rearrange("p (k n) -> p k n", k=KD)
        eT = xin[:].rearrange("p b t n -> p b (t n)").rearrange("p b (i g h) -> p b i g h", i=4, g=4)
        crow, chi = xin[0:2, 0, 0, :], xin[0:2, 0, 1, :]
        lgT = flat[:, 0:1024].rearrange("p (r n) -> p r n", r=2)

        x_rows = x.rearrange("b (t p) d -> p (b t) d", p=P)
        out_rows = out.rearrange("b (t p) d -> p (b t) d", p=P)
        xs_rows = xs.rearrange("(n p) d -> p n d", p=P)
        ys_rows = ys.rearrange("(n p) d -> p n d", p=P)
        xs_zero = xs.rearrange("(p n) d -> p n d", p=P)

        C_POOL, C_HEAD = 0, D
        C_FOLD = C_HEAD + KD * NH
        C_MAX, C_SUM, C_SB = C_FOLD + KD * 32, C_FOLD + KD * 32 + 1, C_FOLD + KD * 32 + 2

        x_loaded = [sem(f"x_loaded{c}") for c in range(NC)]
        cst_loaded, att_loaded, bt_loaded = sem("cst_loaded"), sem("att_loaded"), sem("bt_loaded")
        raw_loaded = [sem("raw_loaded0"), sem("raw_loaded1")]
        b_loaded = [sem("b_loaded0"), sem("b_loaded1")]
        w_hi = [sem("w1_hi"), sem("w2_hi")]
        w_lo = [sem("w1_lo"), sem("w2_lo")]
        xhi_ready, xlo_ready = sem("xhi_ready"), sem("xlo_ready")
        hhi_ready, hlo_ready, rank_read = sem("hhi_ready"), sem("hlo_ready"), sem("rank_read")
        xin_loaded = [sem("xin_loaded0"), sem("xin_loaded1")]
        y_stored = [sem("y_stored0"), sem("y_stored1")]
        zero_made, zero_filled = sem("zero_made"), sem("zero_filled")
        dve_step, pool_step = sem("dve_step"), sem("pool_step")
        var_ready, rstd_ready = sem("var_ready"), sem("rstd_ready")
        nmr_ready, xn_even, xn_odd = sem("nmr_ready"), sem("xn_even"), sem("xn_odd")
        xnT_ps, xnT_ready = sem("xnT_ps"), sem("xnT_ready")
        fold_ps, fold_sb = sem("fold_ps"), sem("fold_sb")
        rowmax_ready, rowmaxT_ps, headmax_ready = sem("rowmax_ready"), sem("rowmaxT_ps"), sem("headmax_ready")
        max_ps = sem("max_ps")
        score_ps, bias_ready, prob_ready = sem("score_ps"), sem("bias_ready"), sem("prob_ready")
        pooled_div, pooledT_ps = sem("pooled_div"), sem("pooledT_ps")
        rsum_ready, probT_ps, probT_ready = sem("rsum_ready"), sem("probT_ps"), sem("probT_ready")
        pooled_ps, pooled_sb = sem("pooled_ps"), sem("pooled_sb")
        headed_ps, headed_sb = sem("headed_ps"), sem("headed_sb")
        mix_ready, m_ps, m_ready, crow_ready = sem("mix_ready"), sem("m_ps"), sem("m_ready"), sem("crow_ready")
        proj_ps, x1_ready = sem("proj_ps"), sem("x1_ready")
        var2_ready, zscale_ready = sem("var2_ready"), sem("zscale_ready")
        z_even, z_odd, zT_ps, zT_ready = sem("z_even"), sem("z_odd"), sem("zT_ps"), sem("zT_ready")
        nmr2_ready = sem("nmr2_ready")
        logits_sb, lgT_ps = sem("logits_sb"), sem("lgT_ps")
        logits_ps, el_ready, onehot_ready = sem("logits_ps"), sem("el_ready"), sem("onehot_ready")
        rank_ps, routed = sem("rank_ps"), sem("routed")
        scattered = sem("scattered")
        up_ps, hid_ready, down_done, out_done = sem("up_ps"), sem("hid_ready"), sem("down_done"), sem("out_done")
        blkT_ps = sem("blkT_ps")
        bias_added, combined_half = sem("bias_added"), sem("combined_half")
        gathered = [sem(f"gathered{r}") for r in range(RING)]
        combined, out_stored = sem("combined"), sem("out_stored")

        GS2 = SA + NB
        early_tiles = list(range(2 * SA))
        steps = []
        for i in range(SZ + 1):
            done = [2 * (SA + i - 1), 2 * (SA + i - 1) + 1] if i else []
            steps.append(early_tiles[2 * SA * i // SZ:2 * SA * (i + 1) // SZ] + done)
        order = [t for step in steps for t in step]

        block = ctx.enter_context(nc.Block())

        @block.sync
        def _(sp):
            def load_x(c):
                sp.dma_start(x_sb[:, c * CH:(c + 1) * CH, :],
                             x_rows[:, c * CH:(c + 1) * CH, :]).then_inc(x_loaded[c], 16)

            load_x(0)
            load_x(1)
            sp.dma_start(cst[:, :], consts).then_inc(cst_loaded, 16)
            load_x(2)
            load_x(3)
            sp.dma_start(att[:, :], attn).then_inc(att_loaded, 16)
            sp.dma_start(nw[:, :], norm).then_inc(att_loaded, 16)
            for c in range(4, NC):
                load_x(c)
            sp.dma_start(bt_bc[:, :], bt.to_broadcast([P, D])).then_inc(bt_loaded, 16)

            def matrix(u, h, e):
                if not (isinstance(u, int) and u == 0):
                    sp.wait_ge(w_lo[h], u)
                src = wpack[e] if isinstance(e, int) else wpack[bass.ds(e, 1)].rearrange("a p n -> (a p) n")
                sp.dma_start(raw[:, h, :], src[:, h * W2:(h + 1) * W2]).then_inc(raw_loaded[h], 16)

            def biases(us, e):
                if isinstance(e, int):
                    one, two = b1pack[e], b2pack[e:e + 1, :]
                else:
                    one, two = b1pack[bass.ds(e, 1)].rearrange("a p n -> (a p) n"), b2pack[bass.ds(e, 1), :]
                sp.dma_start(b1[:, us, :], one).then_inc(b_loaded[us], 16)
                sp.dma_start(b2[:, us, :], two.to_broadcast([P, D])).then_inc(b_loaded[us], 16)

            def shared_rows(g, gs, i):
                sp.dma_start(xin[:, gs, :, :], z_sb[:, bass.ds(2 * i, 2), :]).then_inc(xin_loaded[gs], 16)

            def block_rows(j, gs):
                sp.dma_start(xin[:, gs, :, :], xs_rows[:, bass.ds(2 * j, 2), :]).then_inc(xin_loaded[gs], 16)

            def store(j, s):
                sp.dma_start(ys_rows[:, bass.ds(2 * j, 2), :], yo[:, s, :, :]).then_inc(y_stored[s], 16)

            matrix(0, 0, E)
            matrix(0, 1, E)
            biases(0, E)
            sp.wait_ge(zero_made, 1)
            sp.dma_start(xs_zero, zero[:].rearrange("p (o d) -> p o d", o=1).to_broadcast([P, 2 * NB, D])).then_inc(zero_filled, 16)
            sp.wait_ge(z_even, (NT // 2 + CH) // 2)
            sp.wait_ge(z_odd, (NT // 2 + CH) // 2)
            shared_rows(0, 0, 0)
            shared_rows(1, 1, 1)
            for g in range(2, SA):
                if g == 5:
                    sp.wait_ge(routed, 1)
                    e = sp.value_load(eid[0:1, 0:1], min_val=0, max_val=E - 1)
                    matrix(1, 0, e)
                    matrix(1, 1, e)
                    biases(1, e)
                sp.wait_ge(blkT_ps, g - 1)
                shared_rows(g, g % 2, g)

            def prepare(j, s, turned=True):
                sp.wait_ge(blkT_ps, SA + j - 1)
                block_rows(j, 1 - s)
                if isinstance(j, int) and j == 0:
                    return
                e = sp.value_load(eid[0:1, bass.ds(j, 1)], min_val=0, max_val=E - 1)
                matrix(j + 1, 0, e)
                matrix(j + 1, 1, e)
                sp.wait_ge(out_done, SA + j - 1)
                if isinstance(j, int) and j == 1:
                    sp.wait_ge(bias_added, SA)
                biases(1 - s, e)
                if not (isinstance(j, int) and j < 2):
                    store(j - 2, s)

            sp.wait_ge(scattered, 16 * 2 * NT)
            for j in range(3):
                prepare(j, j % 2)
            with sp.Fori(0, (NB - 3) // 6) as i:
                for q in range(6):
                    prepare(6 * i + 3 + q, (3 + q) % 2)
            for i in range(SZ):
                g = GS2 + i
                sp.wait_ge(blkT_ps, g - 1)
                shared_rows(g, g % 2, SA + i)
                if i == 0:
                    matrix(NB + 1, 0, E)
                    matrix(NB + 1, 1, E)
                if i < 2:
                    sp.wait_ge(out_done, g - 1)
                    if i == 0:
                        biases(0, E)
                    store(NB - 2 + i, (NB + i) % 2)

            for n in range(NT):
                t = order[n]
                if order.index(t ^ 1) < n:
                    t -= t % 2
                    sp.wait_ge(combined, n + 1)
                    sp.dma_start(out_rows[:, t:t + 2, :], x_sb[:, t:t + 2, :]).then_inc(out_stored, 16)
            sp.wait_ge(out_stored, 16 * NT // 2)

        @block.gpsimd
        def _(pool):
            nc.gpsimd.memset(zero[:], 0.0).then_inc(zero_made, 1)
            nc.gpsimd.memset(half[:], -0.5).then_inc(pool_step, 1)
            pool.wait_ge(pool_step, 1)
            for c in range(NC):
                a, z = c * CH, (c + 1) * CH
                pool.wait_ge(var_ready, c + 1)
                nc.gpsimd.tensor_tensor(rstd[:, a:z], vare[:, a:z], half[:], ALU.pow).then_inc(rstd_ready, 1)
            for c in range(NC):
                a, z = c * CH, (c + 1) * CH
                pool.wait_ge(var2_ready, c + 1)
                nc.gpsimd.tensor_tensor(zscale[:, a:z], vare[:, a:z], half[:], ALU.pow).then_inc(zscale_ready, 1)
            pool.wait_ge(zero_filled, 16)
            pool.wait_ge(routed, 1)
            for t in range(NT):
                for k in range(2):
                    nc.gpsimd.indirect_dma_start(
                        xs, bass.IndirectOffsetOnAxis(pos[:, k, t:t + 1], 0), z_sb[:, t, :], None
                    ).then_inc(scattered, 16)
            pool.wait_ge(y_stored[0], 16 * ((NB + 1) // 2))
            pool.wait_ge(y_stored[1], 16 * (NB // 2))
            for n, t in enumerate(order):
                q = n % RING
                if n >= RING:
                    pool.wait_ge(combined, n + 1 - RING)
                for k in range(2):
                    nc.gpsimd.indirect_dma_start(
                        ring[:, q, k, :], None, ys, bass.IndirectOffsetOnAxis(pos[:, k, t:t + 1], 0)
                    ).then_inc(gathered[q], 16)

        @block.tensor
        def _(pe):
            mm = nc.tensor.matmul

            def turn_rows(q):
                pe.wait_ge(xn_even, q + 1)
                pe.wait_ge(xn_odd, q + 1)
                if q >= 2:
                    pe.wait_ge(xnT_ready, q - 1)
                for tt in range(2):
                    for k in range(KD):
                        last = nc.tensor.transpose(psT[:, q % 2, k * 256 + tt * P:k * 256 + (tt + 1) * P],
                                                   z_sb[:, 2 * q + tt, k * P:(k + 1) * P], ident)
                last.then_inc(xnT_ps, 1)

            def fold_query():
                pe.wait_ge(att_loaded, 32)
                for k in range(KD):
                    for n in range(KD):
                        mm(psD[:, 0, C_FOLD + 32 * k:C_FOLD + 32 * k + 32], wqT[:, n, k * P:(k + 1) * P], wqa[:, n, :],
                           start=(n == 0), stop=(n == KD - 1))
                for g in range(4):
                    for n in range(KD):
                        last = mm(psD[32 * g:32 * g + 32, 0, C_SB:C_SB + 1], wqa[:, n, :],
                                  att[:, A_BQ + n:A_BQ + n + 1], start=(n == 0), stop=(n == KD - 1))
                last.then_inc(fold_ps, 1)

            def fold_key(b):
                pe.wait_ge(headed_sb, b + 1)
                for k in range(KD):
                    for n in range(KD):
                        mm(psD[:, b, C_FOLD + 32 * k:C_FOLD + 32 * k + 32], wkT[:, n, k * P:(k + 1) * P], gk[:, n, b, :],
                           start=(n == 0), stop=(n == KD - 1))
                for g in range(4):
                    for n in range(KD):
                        last = mm(psD[32 * g:32 * g + 32, b, C_SB:C_SB + 1], gk[:, n, b, :],
                                  att[:, A_BK + n:A_BK + n + 1], start=(n == 0), stop=(n == KD - 1))
                last.then_inc(fold_ps, 1)

            def score(i):
                r, b = divmod(i, B)
                if r == 0:
                    pe.wait_ge(fold_sb, 1)
                    pe.wait_ge(xnT_ready, (b + 1) * NT // 4)
                else:
                    pe.wait_ge(fold_sb, b + 2)
                for k in range(KD):
                    for g in range(4):
                        n = 4 * b + g
                        last = mm(psU[32 * g:32 * g + 32, b, :], aq[:, k, :] if r == 0 else bk_[:, b, k, :],
                                  xT[:, k, n * 512:(n + 1) * 512], start=(k == 0), stop=(k == KD - 1))
                last.then_inc(score_ps, 1)

            def turn_max(i):
                pe.wait_ge(rowmax_ready, i + 1)
                nc.tensor.transpose(psD[0:1, i % B, 0:P], small[:, i % B, 1:2], ident).then_inc(rowmaxT_ps, 1)

            def spread_max(i):
                pe.wait_ge(headmax_ready, i + 1)
                for g in range(4):
                    last = mm(psD[32 * g:32 * g + 32, i % B, C_MAX:C_MAX + 1], mrow[0:1, i % B, :], ones[0:1, 0:1],
                              start=True, stop=True)
                last.then_inc(max_ps, 1)

            def turn_probs(i):
                b = i % B
                pe.wait_ge(prob_ready, i + 1)
                for j in range(4):
                    last = nc.tensor.transpose(psU[:, 2 + b, j * P:(j + 1) * P], prob[:, b, j * P:(j + 1) * P], ident)
                last.then_inc(probT_ps, 1)

            def pool_rows(i):
                b = i % B
                pe.wait_ge(probT_ready, i + 1)
                for j in range(4):
                    for g in range(4):
                        mm(psD[32 * g:32 * g + 32, b, C_POOL:C_POOL + D], eT[:, b, j, g, :],
                           z_sb[:, b * (S // P) + 4 * g + j, :], start=(j == 0), stop=(j == 3))
                mm(psD[:, b, C_SUM:C_SUM + 1], sel, small[:, b, 5:6], start=True, stop=True).then_inc(pooled_ps, 1)

            def turn_pooled(i):
                b = i % B
                pe.wait_ge(pooled_div, i + 1)
                for k in range(KD):
                    last = nc.tensor.transpose(psD[:, b, C_POOL + k * P:C_POOL + (k + 1) * P],
                                               pooled[:, b, k * P:(k + 1) * P], ident)
                last.then_inc(pooledT_ps, 1)

            def project_pooled(i):
                r, b = divmod(i, B)
                pe.wait_ge(pooled_sb, i + 1)
                wmat = (wq, wk)[r]
                for n in range(KD):
                    for k in range(KD):
                        last = mm(psD[:, b, C_HEAD + NH * n:C_HEAD + NH * (n + 1)], wmat[:, k, n * P:(n + 1) * P],
                                  pool_sb[:, b, k, :], start=(k == 0), stop=(k == KD - 1))
                last.then_inc(headed_ps, 1)

            def mix(b):
                pe.wait_ge(mix_ready, b + 1)
                for k in range(KD):
                    for n in range(KD):
                        mm(psU[:, b, k * D:(k + 1) * D], wqT[:, n, k * P:(k + 1) * P], gt[:, b, n, :],
                           start=(n == 0), stop=(n == KD - 1))
                for n in range(KD):
                    last = mm(psD[0:32, b, 0:D], bqrep[:, n, :], gt[:, b, n, :], start=(n == 0), stop=(n == KD - 1))
                last.then_inc(m_ps, 1)

            proj_bank = [(0, 2)[q % 2] if q < NT // 4 else (1, 3, 0, 2)[q % 4] for q in range(NT // 2)]

            def project(q):
                before = [p for p in range(q) if proj_bank[p] == proj_bank[q]]
                if before:
                    pe.wait_ge(x1_ready, before[-1] + 1)
                b = 2 * q // (NT // B)
                if q % (NT // 4) == 0:
                    pe.wait_ge(m_ready, b + 1)
                    pe.wait_ge(crow_ready, b + 1)
                for tt in range(2):
                    t = 2 * q + tt
                    dst = psU[:, proj_bank[q], tt * D:(tt + 1) * D]
                    for k in range(KD):
                        mm(dst, xT[:, k, t * P:(t + 1) * P], mt[:, b, k, :], start=(k == 0), stop=False)
                    last = mm(dst, one2[:, :], cpair[:, b, :], start=False, stop=True)
                last.then_inc(proj_ps, 1)

            def turn_z(q):
                pe.wait_ge(z_even, q + 1)
                pe.wait_ge(z_odd, q + 1)
                if q >= 2:
                    pe.wait_ge(zT_ready, q - 1)
                for tt in range(2):
                    for k in range(KD):
                        last = nc.tensor.transpose(psT[:, q % 2, k * 256 + tt * P:k * 256 + (tt + 1) * P],
                                                   z_sb[:, 2 * q + tt, k * P:(k + 1) * P], ident)
                last.then_inc(zT_ps, 1)

            def router(b):
                pe.wait_ge(zT_ready, (b + 1) * NT // 4)
                for k in range(KD):
                    for g in range(4):
                        n = 4 * b + g
                        last = mm(psD[32 * g:32 * g + 32, b, :], rwT[:, k, :], xT[:, k, n * 512:(n + 1) * 512],
                                  start=(k == 0), stop=(k == KD - 1))
                last.then_inc(logits_ps, 1)

            def project_chunk(c):
                project(2 * c)
                project(2 * c + 1)

            def turn_chunk(c):
                turn_z(2 * c)
                turn_z(2 * c + 1)

            pe.wait_ge(cst_loaded, 16)
            for q in range(4):
                turn_rows(q)
            fold_query()
            for q in range(4, 8):
                turn_rows(q)
            score(0)
            turn_rows(8)
            turn_rows(9)
            turn_rows(10)
            turn_rows(11)
            turn_max(0)
            turn_rows(12)
            turn_rows(13)
            spread_max(0)
            turn_probs(0)
            turn_rows(14)
            turn_rows(15)
            pool_rows(0)
            score(1)
            turn_pooled(0)
            project_pooled(0)
            turn_max(1)
            fold_key(0)
            spread_max(1)
            score(2)
            turn_probs(1)
            turn_max(2)
            pool_rows(1)
            spread_max(2)
            turn_pooled(1)
            turn_probs(2)
            project_pooled(1)
            pool_rows(2)
            fold_key(1)
            turn_pooled(2)
            score(3)
            project_pooled(2)
            turn_max(3)
            mix(0)
            spread_max(3)
            project_chunk(0)
            turn_probs(3)
            pool_rows(3)
            project_chunk(1)
            turn_pooled(3)
            project_chunk(2)
            turn_chunk(0)
            project_pooled(3)
            project_chunk(3)
            turn_chunk(1)
            mix(1)
            for c in range(4, NC + 2):
                if c < NC:
                    project_chunk(c)
                if c == NC // 2 + 2:
                    router(0)
                turn_chunk(c - 2)
            router(1)

            def ranks():
                pe.wait_ge(onehot_ready, 1)
                ohf = oh[:].rearrange("p t e -> p (t e)")
                mm(psD[:, 1, 0:NT * E], tri, ohf, start=True, stop=True)
                mm(psD[:, 1, NT * E:2 * NT * E], ones, ohf, start=True, stop=True).then_inc(rank_ps, 1)

            def turn(g, gs, uses):
                pe.wait_ge(xin_loaded[gs], 16 * uses)
                for half in range(2):
                    for k in range(KD):
                        last = nc.tensor.transpose(psT[:, gs, k * BLK + half * P:k * BLK + (half + 1) * P],
                                                   xin[:, gs, half, k * P:(k + 1) * P], ident)
                last.then_inc(blkT_ps, 1)

            def up(g, gs, slot):
                pe.wait_ge(xlo_ready, g + 1)
                for m in range(MH):
                    for k in range(KD):
                        col = slice(k * H + m * P, k * H + (m + 1) * P)
                        dst = psU[:, m // 2, (m % 2) * BLK:(m % 2 + 1) * BLK]
                        mm(dst, whi[:, slot, col], xhi[:, gs, k, :], start=(k == 0), stop=False)
                        mm(dst, whi[:, slot, col], xlo[:, gs, k, :], start=False, stop=False)
                        last = mm(dst, wlo[:, slot, col], xhi[:, gs, k, :], start=False, stop=(k == KD - 1))
                    if m % 2:
                        last.then_inc(up_ps, 1)

            def down(g, gs, slot):
                if not (isinstance(g, int) and g < 2):
                    pe.wait_ge(out_done, g - 1)
                for half in range(2):
                    for c in range(MH):
                        if half == 0 and c % 2 == 0:
                            pe.wait_ge(hlo_ready, g * (MH // 2) + c // 2 + 1)
                        rows = slice(half * P, (half + 1) * P)
                        col = slice(c * D, (c + 1) * D)
                        dst = psD[:, gs, half * D:(half + 1) * D]
                        mm(dst, hhi[:, c, rows], whi[:, slot, col], start=(c == 0), stop=False)
                        mm(dst, hhi[:, c, rows], wlo[:, slot, col], start=False, stop=False)
                        last = mm(dst, hlo[:, c, rows], whi[:, slot, col], start=False, stop=(c == MH - 1))
                last.then_inc(down_done, 1)

            def tile(g, gs, u, um, uses=None, fresh=True):
                if fresh:
                    pe.wait_ge(w_lo[0], u + 1)
                up(g, gs, 2 * um % 3)
                if uses is not None:
                    turn(g + 1, 1 - gs, uses)
                if isinstance(g, int) and g == 1:
                    ranks()
                    pe.wait_ge(rank_read, 1)
                if fresh:
                    pe.wait_ge(w_lo[1], u + 1)
                down(g, gs, (2 * um + 1) % 3)

            pe.wait_ge(zT_ready, NT // 2)
            turn(0, 0, 1)
            turn(1, 1, 1)
            for r in range(2):
                pe.wait_ge(logits_sb, r + 1)
                for i in range(4):
                    last = nc.tensor.transpose(psU[:, r, i * P:(i + 1) * P], lgT[:, r, i * P:(i + 1) * P], ident)
                last.then_inc(lgT_ps, 1)
            pe.wait_ge(el_ready, 2)
            tile(0, 0, 0, 0)
            tile(1, 1, 0, 0, 2, False)
            with pe.Fori(1, SA // 2) as i:
                tile(2 * i, 0, 0, 0, i + 1, False)
                tile(2 * i + 1, 1, 0, 0, i + 2, False)
            tile(SA - 1, 0, 0, 0, (SA + 1) // 2, False)
            for j in range(3):
                g = SA + j
                tile(g, g % 2, j + 1, (j + 1) % 3, (g + 1) // 2 + 1)
            with pe.Fori(0, (NB - 3) // 6) as i:
                for q in range(6):
                    tile(6 * i + SA + 3 + q, (SA + 3 + q) % 2, 6 * i + 4 + q, (4 + q) % 3,
                         3 * i + (SA + 4 + q) // 2 + 1)
            for i in range(SZ):
                g = GS2 + i
                tile(g, g % 2, NB + 1, (NB + 1) % 3, (g + 1) // 2 + 1 if i < SZ - 1 else None, i == 0)

        @block.scalar
        def _(act):
            copy = ACT.Copy
            def rows_out(q):
                act.wait_ge(xnT_ps, q + 1)
                nc.scalar.activation(xT[:, :, q * 256:(q + 1) * 256],
                                     psT[:, q % 2, :].rearrange("p (k n) -> p k n", k=KD),
                                     copy).then_inc(xnT_ready, 1)

            for c in range(NC):
                act.wait_ge(nmr_ready, c + 1)
                for t in range(c * CH + 1, (c + 1) * CH, 2):
                    nc.scalar.activation(z_sb[:, t, :], x_sb[:, t, :], ACT.Identity, bias=nmr[:, t:t + 1],
                                         scale=rstd[:, t:t + 1]).then_inc(xn_odd, 1)
                if c >= 1:
                    rows_out(2 * c - 2)
                    rows_out(2 * c - 1)

            def split_hi(h, u, slot):
                act.wait_ge(raw_loaded[h], 16 * (u + 1))
                for half in (slice(0, W2 // 2), slice(W2 // 2, W2)):
                    nc.scalar.activation(whi[:, slot, half], raw[:, h, half], copy).then_inc(w_hi[h], 1)

            def exponentials(i):
                b = i % B
                act.wait_ge(bias_ready, i + 1)
                nc.scalar.activation(prob[:, b, :], psU[:, b, :], ACT.Exp, bias=small[:, b, 4:5], scale=SCALE,
                                     accum_out=small[:, b, 5:6]).then_inc(prob_ready, 1)

            def probs_out(i):
                act.wait_ge(probT_ps, i + 1)
                nc.scalar.activation(eT[:, i % B].rearrange("p i g h -> p (i g h)"), psU[:, 2 + i % B, :],
                                     copy).then_inc(probT_ready, 1)

            def pooled_out(i):
                b = i % B
                act.wait_ge(rsum_ready, i + 1)
                nc.scalar.activation(pooled[:, b, :], psD[:, b, C_POOL:C_POOL + D], copy,
                                     scale=small[:, b, 6:7]).then_inc(pooled_div, 1)

            def mix_out(b):
                act.wait_ge(m_ps, b + 1)
                nc.scalar.activation(mt[:, b].rearrange("p k n -> p (k n)"), psU[:, b, :], copy).then_inc(m_ready, 1)

            def z_out(q):
                act.wait_ge(zT_ps, q + 1)
                for k in range(KD):
                    last = nc.scalar.activation(xT[:, k, q * 256:(q + 1) * 256], psT[:, q % 2, k * 256:(k + 1) * 256],
                                                copy, scale=nw[:, k:k + 1])
                last.then_inc(zT_ready, 1)

            def logits_out(r):
                act.wait_ge(logits_ps, r + 1)
                nc.scalar.activation(lgT[:, r, :], psD[:, r, :], copy).then_inc(logits_sb, 1)

            exponentials(0)
            probs_out(0)
            rows_out(14)
            rows_out(15)
            split_hi(0, 0, 0)
            pooled_out(0)
            exponentials(1)
            probs_out(1)
            split_hi(1, 0, 1)
            pooled_out(1)
            exponentials(2)
            probs_out(2)
            pooled_out(2)
            mix_out(0)
            exponentials(3)
            probs_out(3)
            pooled_out(3)
            for c in range(NC):
                if c == 2:
                    mix_out(1)
                act.wait_ge(nmr2_ready, c + 1)
                for t in range(c * CH + 1, (c + 1) * CH, 2):
                    nc.scalar.activation(z_sb[:, t, :], x_sb[:, t, :], ACT.Identity, bias=nmr[:, t:t + 1],
                                         scale=zscale[:, t:t + 1]).then_inc(z_odd, 1)
                z_out(2 * c)
                z_out(2 * c + 1)
                if c == NC // 2:
                    logits_out(0)
            logits_out(1)

            def turned_hi(g, gs):
                act.wait_ge(blkT_ps, g + 1)
                for k in range(KD):
                    last = nc.scalar.activation(xhi[:, gs, k, :], psT[:, gs, k * BLK:(k + 1) * BLK], copy,
                                                scale=nw[:, k:k + 1])
                last.then_inc(xhi_ready, 1)

            def tile(g, gs, us, loads, turn=True, fresh=None):
                first = isinstance(g, int) and g == 0
                act.wait_ge(b_loaded[us], 32 * loads)
                for m in range(MH):
                    if m % 2 == 0:
                        act.wait_ge(up_ps, g * (MH // 2) + m // 2 + 1)
                    last = nc.scalar.activation(hid[:, m, :], psU[:, m // 2, (m % 2) * BLK:(m % 2 + 1) * BLK],
                                                ACT.Relu, bias=b1[:, us, m:m + 1])
                    if m % 2:
                        last.then_inc(hid_ready, 1)
                if turn and not first:
                    turned_hi(g + 1, 1 - gs)
                if fresh is not None:
                    u, um = fresh
                    act.wait_ge(down_done, g)
                    split_hi(0, u, 2 * um % 3)
                    split_hi(1, u, (2 * um + 1) % 3)

            turned_hi(0, 0)
            for r in range(2):
                act.wait_ge(lgT_ps, r + 1)
                nc.scalar.activation(
                    pr[:, r * 16:(r + 1) * 16, :].rearrange("p (g i) e -> p i g e", g=4),
                    psU[:, r, :].rearrange("p (i g e) -> p i g e", i=4, g=4)[:, :, :, 0:E],
                    ACT.Exp, scale=-1.0).then_inc(el_ready, 1)
            turned_hi(1, 1)
            tile(0, 0, 0, 1)
            tile(1, 1, 0, 1)
            act.wait_ge(rank_ps, 1)
            nc.scalar.activation(posm[:], psD[:, 1, 0:NT * E].rearrange("p (t e) -> p e t", e=E), copy)
            nc.scalar.activation(tot[:], psD[:, 1, NT * E:2 * NT * E].rearrange("p (t e) -> p e t", e=E),
                                 copy).then_inc(rank_read, 1)
            with act.Fori(1, SA // 2) as i:
                tile(2 * i, 0, 0, 1)
                tile(2 * i + 1, 1, 0, 1)
            tile(SA - 1, 0, 0, 1, fresh=(1, 1))
            for j in range(3):
                g, u = SA + j, j + 1
                tile(g, g % 2, u % 2, u // 2 + 1, fresh=(u + 1, (u + 1) % 3))
            with act.Fori(0, (NB - 3) // 6) as i:
                for q in range(6):
                    tile(6 * i + SA + 3 + q, (SA + 3 + q) % 2, (4 + q) % 2, 3 * i + (4 + q) // 2 + 1,
                         fresh=(6 * i + 5 + q, (5 + q) % 3))
            for i in range(SZ):
                g = GS2 + i
                tile(g, g % 2, (NB + 1) % 2, (NB + 1) // 2 + 1, i < SZ - 1)

        @block.vector
        def _(dve):
            count = [0]

            def link(ins):
                count[0] += 1
                ins.then_inc(dve_step, 1)
                dve.wait_ge(dve_step, count[0])

            V = nc.vector

            def moments(c, rms, ready):
                a, z = c * CH, (c + 1) * CH
                st = stats[:, a:z, :]
                V.tensor_tensor(ssum[:, a:z], st[:, :, 1], st[:, :, 4], ALU.add)
                V.tensor_tensor(sm2[:, a:z], st[:, :, 2], st[:, :, 5], ALU.add)
                link(V.tensor_tensor(sdif[:, a:z], st[:, :, 1], st[:, :, 4], ALU.subtract))
                V.tensor_scalar(mean[:, a:z], ssum[:, a:z], 0.5, None, ALU.mult)
                V.tensor_scalar(sm2[:, a:z], sm2[:, a:z], 1.0 / D, None, ALU.mult)
                link(V.scalar_tensor_tensor(sdif[:, a:z], sdif[:, a:z], 0.25, sdif[:, a:z], ALU.mult, ALU.mult))
                link(V.tensor_tensor(var[:, a:z], sdif[:, a:z], sm2[:, a:z], ALU.add))
                if not rms:
                    V.tensor_scalar(vare[:, a:z], var[:, a:z], EPS_LN, None, ALU.add).then_inc(ready, 1)
                    return
                link(V.tensor_scalar(vare[:, a:z], var[:, a:z], EPS_LN, None, ALU.add))
                V.scalar_tensor_tensor(vare[:, a:z], vare[:, a:z], EPS_RMS, var[:, a:z],
                                       ALU.mult, ALU.add).then_inc(ready, 1)

            def normalise(c):
                dve.wait_ge(rstd_ready, c + 1)
                a, z = c * CH, (c + 1) * CH
                V.scalar_tensor_tensor(nmr[:, a:z], mean[:, a:z], -1.0, rstd[:, a:z],
                                       ALU.mult, ALU.mult).then_inc(nmr_ready, 1)
                for t in range(a, z, 2):
                    V.tensor_scalar(z_sb[:, t, :], x_sb[:, t, :], mean[:, t:t + 1], rstd[:, t:t + 1],
                                    ALU.subtract, ALU.mult).then_inc(xn_even, 1)

            def row_max(i):
                dve.wait_ge(score_ps, i + 1)
                V.tensor_reduce(small[:, i % B, 1:2], psU[:, i % B, :], X, ALU.max).then_inc(rowmax_ready, 1)

            def head_max(i):
                dve.wait_ge(rowmaxT_ps, i + 1)
                V.tensor_reduce(mrow[0:1, i % B, :], psD[0:1, i % B, 0:P].rearrange("p (g h) -> p h g", g=4), X,
                                ALU.max).then_inc(headmax_ready, 1)

            def softmax_bias(i):
                b = i % B
                dve.wait_ge(max_ps, i + 1)
                dve.wait_ge(fold_sb, 1 if i < B else 2 + b)
                link(V.tensor_tensor(small[:, b, 2:3], psD[:, b, C_MAX:C_MAX + 1], small[:, b, 0:1], ALU.add))
                link(V.tensor_tensor(small[:, b, 3:4], small[:, b, 0:1], small[:, b, 2:3], ALU.subtract))
                V.tensor_scalar(small[:, b, 4:5], small[:, b, 3:4], SCALE, None, ALU.mult).then_inc(bias_ready, 1)

            for c in range(NC):
                dve.wait_ge(x_loaded[c], 16)
                for t in range(c * CH, (c + 1) * CH):
                    last = V.bn_stats(stats[:, t, :], x_sb[:, t, :])
                link(last)
                moments(c, False, var_ready)
                if c >= 1:
                    normalise(c - 1)
                if c == 3:
                    dve.wait_ge(fold_ps, 1)
                    V.tensor_copy(aq[:].rearrange("p k h -> p (k h)"), psD[:, 0, C_FOLD:C_FOLD + KD * 32])
                    for b in range(B):
                        last = V.tensor_tensor(small[:, b, 0:1], psD[:, 0, C_SB:C_SB + 1], att[:, A_BQA:A_BQA + 1], ALU.add)
                    last.then_inc(fold_sb, 1)
                    link(V.tensor_reduce(own, ident.rearrange("p (g h) -> p h g", g=4), X, ALU.add))
                    V.tensor_copy(sel.rearrange("p (g h) -> p g h", g=4),
                                  own.rearrange("p (o h) -> p o h", o=1).to_broadcast([P, 4, 32]))
                    for n in range(KD):
                        V.tensor_scalar(bqrep[:, n, :], ones[:, 0:32], att[:, A_BQ + n:A_BQ + n + 1], None, ALU.mult)
                if c == NC - 2:
                    row_max(0)
                if c == NC - 1:
                    head_max(0)
            normalise(NC - 1)
            softmax_bias(0)
            dve.wait_ge(bt_loaded, 16)

            def split_lo(h, u, slot):
                for n, half in enumerate((slice(0, W2 // 2), slice(W2 // 2, W2))):
                    dve.wait_ge(w_hi[h], 2 * u + n + 1)
                    last = V.tensor_tensor(wlo[:, slot, half], raw[:, h, half], whi[:, slot, half].bitcast(F32),
                                           ALU.subtract)
                last.then_inc(w_lo[h], 1)

            def reciprocal_sum(i):
                dve.wait_ge(pooled_ps, i + 1)
                V.reciprocal(small[:, i % B, 6:7], psD[:, i % B, C_SUM:C_SUM + 1]).then_inc(rsum_ready, 1)

            def add_groups(i):
                b = i % B
                dve.wait_ge(pooledT_ps, i + 1)
                V.tensor_reduce(pool_sb[:, b], psD[:, b, C_POOL:C_POOL + D]
                                .rearrange("p (k g h) -> p k h g", k=KD, g=4)[:, :, 0:NH, :], X,
                                ALU.add).then_inc(pooled_sb, 1)

            def own_head(i):
                b = i % B
                dve.wait_ge(headed_ps, i + 1)
                link(V.tensor_tensor(dtmp[:, b], psD[:, b, C_HEAD:C_HEAD + KD * NH].rearrange("p (n h) -> p n h", n=KD),
                                     hm, ALU.mult))
                link(V.tensor_reduce(dred[:, b, :], dtmp[:, b], X, ALU.add))

            def pooled_query(b):
                own_head(b)
                link(V.tensor_tensor(pq[:, b, :], dred[:, b, :], att[:, A_BQ:A_BQ + KD], ALU.add))
                for n in range(KD):
                    last = V.tensor_scalar(gk[:, n, b, :], wka[:, n, :], pq[:, b, n:n + 1], None, ALU.mult)
                last.then_inc(headed_sb, 1)

            def folded_key(b):
                dve.wait_ge(fold_ps, b + 2)
                V.tensor_copy(bk_[:, b].rearrange("p k h -> p (k h)"), psD[:, b, C_FOLD:C_FOLD + KD * 32])
                V.tensor_tensor(small[:, b, 0:1], psD[:, b, C_SB:C_SB + 1], att[:, A_BKA:A_BKA + 1],
                                ALU.add).then_inc(fold_sb, 1)

            def pooled_key(b):
                own_head(B + b)
                link(V.tensor_tensor(dred[:, b, :], dred[:, b, :], att[:, A_BK:A_BK + KD], ALU.add))
                link(V.tensor_tensor(pk[:, b, :], dred[:, b, :], pq[:, b, :], ALU.mult))
                for n in range(KD):
                    last = V.scalar_tensor_tensor(gt[:, b, n, :], wt[:, n, :], pk[:, b, n:n + 1], eye[:, n, :],
                                                  ALU.mult, ALU.add)
                last.then_inc(mix_ready, 1)

            def bias_row(b):
                dve.wait_ge(m_ps, b + 1)
                link(V.tensor_tensor(crow, psD[0:2, b, 0:D], bt_bc[0:2, :], ALU.add))
                link(V.tensor_copy(chi.bitcast(F32R), crow))
                V.scalar_tensor_tensor(cpair[:, b, :], chi, cst[0:2, C_HILO:C_HILO + 1], crow,
                                       ALU.mult, ALU.add).then_inc(crow_ready, 1)

            def project_chunk(c):
                for q in (2 * c, 2 * c + 1):
                    dve.wait_ge(proj_ps, q + 1)
                    pair = x_sb[:, 2 * q:2 * q + 2, :]
                    V.tensor_tensor(pair, psU[:, (0, 2)[q % 2] if q < NT // 4 else (1, 3, 0, 2)[q % 4], :]
                                    .rearrange("p (t n) -> p t n", t=2), pair, ALU.add).then_inc(x1_ready, 1)
                    dve.wait_ge(x1_ready, q + 1)
                    for t in (2 * q, 2 * q + 1):
                        last = V.bn_stats(stats[:, t, :], x_sb[:, t, :])
                link(last)
                moments(c, True, var2_ready)

            def normalise_chunk(c):
                dve.wait_ge(zscale_ready, c + 1)
                a, z = c * CH, (c + 1) * CH
                V.scalar_tensor_tensor(nmr[:, a:z], mean[:, a:z], -1.0, zscale[:, a:z],
                                       ALU.mult, ALU.mult).then_inc(nmr2_ready, 1)
                for t in range(a, z, 2):
                    V.tensor_scalar(z_sb[:, t, :], x_sb[:, t, :], mean[:, t:t + 1], zscale[:, t:t + 1],
                                    ALU.subtract, ALU.mult).then_inc(z_even, 1)

            V.tensor_copy(one2[:], ones[0:2, :])
            split_lo(0, 0, 0)
            reciprocal_sum(0)
            row_max(1)
            add_groups(0)
            pooled_query(0)
            head_max(1)
            folded_key(0)
            softmax_bias(1)
            row_max(2)
            head_max(2)
            reciprocal_sum(1)
            softmax_bias(2)
            add_groups(1)
            split_lo(1, 0, 1)
            pooled_query(1)
            reciprocal_sum(2)
            folded_key(1)
            add_groups(2)
            row_max(3)
            pooled_key(0)
            head_max(3)
            bias_row(0)
            softmax_bias(3)
            project_chunk(0)
            reciprocal_sum(3)
            project_chunk(1)
            add_groups(3)
            normalise_chunk(0)
            project_chunk(2)
            pooled_key(1)
            normalise_chunk(1)
            project_chunk(3)
            bias_row(1)
            normalise_chunk(2)
            for c in range(4, NC + 1):
                if c < NC:
                    project_chunk(c)
                normalise_chunk(c - 1)

            def turned_lo(g, gs):
                dve.wait_ge(xhi_ready, g + 1)
                for k in range(KD):
                    last = V.scalar_tensor_tensor(xlo[:, gs, k, :], psT[:, gs, k * BLK:(k + 1) * BLK],
                                                  nw[:, k:k + 1], xhi[:, gs, k, :].bitcast(F32),
                                                  ALU.mult, ALU.subtract)
                last.then_inc(xlo_ready, 1)

            def hidden(g):
                for b in range(MH // 2):
                    two = slice(2 * b, 2 * b + 2)
                    n = g * (MH // 2) + b + 1
                    dve.wait_ge(hid_ready, n)
                    V.tensor_copy(hhi[:, two, :], hid[:, two, :]).then_inc(hhi_ready, 1)
                    dve.wait_ge(hhi_ready, n)
                    V.tensor_tensor(hlo[:, two, :], hid[:, two, :], hhi[:, two, :].bitcast(F32),
                                    ALU.subtract).then_inc(hlo_ready, 1)

            def shared_out(g, gs, t):
                dve.wait_ge(down_done, g + 1)
                pair = x_sb[:, bass.ds(t, 2), :]
                V.tensor_tensor(pair, psD[:, gs, :].rearrange("p (t n) -> p t n", t=2), pair,
                                ALU.add).then_inc(out_done, 1)
                dve.wait_ge(out_done, g + 1)
                return V.tensor_tensor(pair, pair, b2[:, 0:1, :].to_broadcast([P, 2, D]), ALU.add)

            def over_e(ap):
                return ap.rearrange("p (t o) -> p t o", o=1).to_broadcast([P, NT, E])

            def line(tensor):
                return tensor[:].rearrange("p t e -> p (t e)")

            turned_lo(0, 0)
            dve.wait_ge(el_ready, 2)
            link(V.tensor_scalar(line(pr), line(pr), 1.0, None, ALU.add))
            link(V.reciprocal(line(pr), line(pr)))

            def best(src, row, onehot):
                link(V.tensor_reduce(top[:, row, :], src[:], X, ALU.max))
                link(V.tensor_tensor(ra[:], src[:], over_e(top[:, row, :]), ALU.is_equal))
                link(V.scalar_tensor_tensor(line(ra), line(ra), -float(E), iota.rearrange("p t e -> p (t e)"),
                                            ALU.mult, ALU.add))
                link(V.tensor_reduce(top[:, row + 1, :], ra[:], X, ALU.min))
                link(V.tensor_scalar(top[:, row + 1, :], top[:, row + 1, :], float(E), None, ALU.add))
                link(V.tensor_tensor(onehot[:], iota, over_e(top[:, row + 1, :]), ALU.is_equal))

            best(pr, 0, oh1)
            hidden(0)
            turned_lo(1, 1)
            link(V.scalar_tensor_tensor(line(pr2), line(oh1), -2.0, line(pr), ALU.mult, ALU.add))
            best(pr2, 2, oh2)
            V.tensor_tensor(line(oh), line(oh1), line(oh2), ALU.add).then_inc(onehot_ready, 1)
            link(V.tensor_tensor(top[:, 4, :], top[:, 0, :], top[:, 2, :], ALU.add))
            link(V.tensor_scalar(top[:, 4, :], top[:, 4, :], EPS_W, None, ALU.add))
            link(V.reciprocal(top[:, 5, :], top[:, 4, :]))
            V.tensor_tensor(top[:, 6, :], top[:, 0, :], top[:, 5, :], ALU.mult)
            link(V.tensor_tensor(top[:, 7, :], top[:, 2, :], top[:, 5, :], ALU.mult))
            shared_out(0, 0, 0).then_inc(bias_added, 1)
            hidden(1)
            turned_lo(2, 0)
            dve.wait_ge(rank_read, 1)
            link(V.tensor_tensor_scan(inc[:].rearrange("p e t -> p (e t)"), cst[:, C_SCAN:C_SCAN + E * NT],
                                      tot[:].rearrange("p e t -> p (e t)"), 0.0, ALU.mult, ALU.add))
            link(V.tensor_tensor(thr[:], inc[:, :, NT - 1:NT].to_broadcast([P, E, MAXT]),
                                 cst[:, C_THR:C_THR + E * MAXT].rearrange("p (e m) -> p e m", e=E), ALU.is_gt))
            link(V.tensor_reduce(blk[:, 0, :], thr[:], X, ALU.add))
            link(V.tensor_tensor_scan(blk[:, 1, :], ones[:, 0:E], blk[:, 0, :], 0.0, ALU.mult, ALU.add))
            link(V.tensor_tensor(blk[:, 2, :], blk[:, 1, :], blk[:, 0, :], ALU.subtract))
            link(V.tensor_scalar(blk[:, 3, :], blk[:, 2, :], float(BLK), None, ALU.mult))
            link(V.tensor_tensor(tot[:], inc[:], tot[:], ALU.subtract))
            link(V.tensor_tensor(posm[:], posm[:], tot[:], ALU.add))
            link(V.tensor_tensor(posm[:], posm[:],
                                 blk[:, 3, :].rearrange("p (e o) -> p e o", o=1).to_broadcast([P, E, NT]), ALU.add))
            for k, (onehot, prod) in enumerate(((oh1, ra), (oh2, pr2))):
                link(V.tensor_tensor(prod[:], onehot[:], posm[:].rearrange("p e t -> p t e"), ALU.mult))
                link(V.tensor_reduce(top[:, 4 + k, :], prod[:], X, ALU.add))
                V.tensor_copy(pos[:, k, :], top[:, 4 + k, :])
            link(V.tensor_tensor(bcmp[:], cst[:, C_BLK:C_BLK + NBP * E].rearrange("p (n e) -> p n e", e=E),
                                 blk[:, 1:2, :].to_broadcast([P, NBP, E]), ALU.is_ge))
            link(V.tensor_reduce(eidf[:], bcmp[:], X, ALU.add))
            link(V.tensor_scalar(eidf[:], eidf[:], float(E - 1), None, ALU.min))
            V.tensor_copy(eid[:], eidf[:]).then_inc(routed, 1)

            def expert_out(j, s, stored, loads):
                dve.wait_ge(down_done, SA + j + 1)
                if stored is not None:
                    dve.wait_ge(y_stored[s], 16 * stored)
                dve.wait_ge(b_loaded[1 - s], 32 * loads)
                V.tensor_tensor(yo[:, s, :, :], psD[:, 1 - s, :].rearrange("p (t n) -> p t n", t=2),
                                b2[:, 1 - s:2 - s, :].to_broadcast([P, 2, D]), ALU.add).then_inc(out_done, 1)

            def fresh(u, um):
                split_lo(0, u, 2 * um % 3)
                split_lo(1, u, (2 * um + 1) % 3)

            with dve.Fori(1, SA // 2) as i:
                shared_out(2 * i - 1, 1, 4 * i - 2).then_inc(bias_added, 1)
                hidden(2 * i)
                turned_lo(2 * i + 1, 1)
                shared_out(2 * i, 0, 4 * i).then_inc(bias_added, 1)
                hidden(2 * i + 1)
                turned_lo(2 * i + 2, 0)
            shared_out(SA - 2, 1, 2 * (SA - 2)).then_inc(bias_added, 1)
            hidden(SA - 1)
            turned_lo(SA, 1)
            fresh(1, 1)
            for j in range(3):
                g, u = SA + j, j + 1
                if j == 0:
                    shared_out(g - 1, (g - 1) % 2, 2 * (g - 1)).then_inc(bias_added, 1)
                else:
                    expert_out(j - 1, (j - 1) % 2, None, (u - 1) // 2 + 1)
                hidden(g)
                turned_lo(g + 1, (g + 1) % 2)
                fresh(u + 1, (u + 1) % 3)
            with dve.Fori(0, (NB - 3) // 6) as i:
                for q in range(6):
                    expert_out(6 * i + 2 + q, q % 2, 3 * i + (2 + q) // 2, 3 * i + (3 + q) // 2 + 1)
                    hidden(6 * i + SA + 3 + q)
                    turned_lo(6 * i + SA + 4 + q, (SA + 4 + q) % 2)
                    fresh(6 * i + 5 + q, (5 + q) % 3)

            def combine(n, k):
                t, q = order[n], n % RING
                dve.wait_ge(combined_half, n + 1) if k else dve.wait_ge(gathered[q], 32 * (n // RING + 1))
                V.scalar_tensor_tensor(x_sb[:, t, :], ring[:, q, k, :], top[:, 6 + k, t:t + 1], x_sb[:, t, :],
                                       ALU.mult, ALU.add).then_inc(combined if k else combined_half, 1)

            n = 0
            for i in range(SZ + 1):
                g = GS2 + i
                if i == 0:
                    expert_out(NB - 1, (NB - 1) % 2, (NB - 1) // 2, NB // 2 + 1)
                else:
                    link(shared_out(g - 1, (g - 1) % 2, 2 * (SA + i - 1)))
                if i < SZ:
                    hidden(g)
                if i < SZ - 1:
                    turned_lo(g + 1, (g + 1) % 2)
                end = n + len(steps[i])
                for n in range(n, end, 2):
                    for k in range(2):
                        for m in range(n, min(n + 2, end)):
                            combine(m, k)
                n = end


def constants():
    c = np.zeros((P, C_ALL), np.float32)
    p = np.arange(P)
    c[:, C_ID:C_ID + P] = np.eye(P)
    c[:, C_TRI:C_TRI + P] = p[:, None] < p[None, :]
    c[:, C_ONE:C_ONE + P] = 1
    c[:, C_EYE:C_EYE + KD * D] = np.eye(D).reshape(KD, P, D).transpose(1, 0, 2).reshape(P, KD * D)
    feature = np.arange(KD)[None, :, None] * P + p[:, None, None]
    c[:, C_HM:C_HM + KD * NH] = (feature // (D // NH) == np.arange(NH)).reshape(P, KD * NH)
    c[:, C_IOTA:C_IOTA + NT * E] = np.tile(np.arange(E), NT)
    c[:, C_SCAN:C_SCAN + E * NT] = np.tile(np.arange(NT) > 0, E)
    c[:, C_THR:C_THR + E * MAXT] = np.tile(np.arange(MAXT) * BLK, E)
    c[:, C_BLK:C_BLK + NBP * E] = np.repeat(np.arange(NBP), E)
    c[1, C_HILO] = -1
    return c


def rows_first(m):
    return np.ascontiguousarray(m.reshape(KD, P, -1).transpose(1, 0, 2).reshape(P, -1))


def kernel(**inputs):
    import concourse.bacc as bacc
    from concourse.bass_utils import run_bass_kernel_spmd

    a = {k: np.asarray(v) for k, v in inputs.items()}
    A, F = "L0_attn_", "L0_ffn_"
    heads = lambda m: np.concatenate([m, np.zeros((D, 32 - NH), np.float32)], 1)
    head_bias = lambda v: np.concatenate([v, np.zeros(32 - NH, np.float32)] * 4)[:, None]
    attn = np.concatenate([
        rows_first(a[A + "Wq"]), rows_first(a[A + "Wk"]), rows_first(a[A + "Wt"]),
        rows_first(a[A + "Wq"].T), rows_first(a[A + "Wk"].T),
        rows_first(heads(a[A + "Wqa"])), rows_first(heads(a[A + "Wka"])),
        rows_first(a[A + "bq"]), rows_first(a[A + "bk"]),
        rows_first(np.concatenate([a[F + "router_w"].T, np.zeros((D, 32 - E), np.float32)], 1)), head_bias(a[A + "bqa"]), head_bias(a[A + "bka"])], 1)
    w1 = np.concatenate([a[F + "ew1"], a[F + "sw1"][None]])
    w2 = np.concatenate([a[F + "ew2"], a[F + "sw2"][None]])
    w1 = w1.reshape(E + 1, KD, P, H).transpose(0, 2, 1, 3).reshape(E + 1, P, W2)
    w2 = w2.reshape(E + 1, MH, P, D).transpose(0, 2, 1, 3).reshape(E + 1, P, W2)
    arrays = {
        "x": a[A + "hidden_states"],
        "consts": constants(),
        "attn": attn,
        "norm": rows_first(a[F + "norm_weight"]),
        "bt": a[A + "bt"][None],
        "wpack": np.concatenate([w1, w2], 2),
        "b1pack": np.concatenate([a[F + "eb1"], a[F + "sb1"][None]]).reshape(E + 1, MH, P).transpose(0, 2, 1),
        "b2pack": np.concatenate([a[F + "eb2"], a[F + "sb2"][None]]),
    }
    nc = bacc.Bacc("TRN2", target_bir_lowering=False, num_devices=1)
    feeds, args = {}, []
    for name, v in arrays.items():
        v = np.ascontiguousarray(v)
        feeds["in_" + name] = v
        args.append(nc.dram_tensor("in_" + name, v.shape, mybir.dt.from_np(v.dtype), kind="ExternalInput").ap())
    out = nc.dram_tensor("out", (B, S, D), F32, kind="ExternalOutput").ap()
    build(nc, *args, out)
    return run_bass_kernel_spmd(nc, [feeds], core_ids=[0]).results[0]["out"]
```
